# Optimizing a Trainium2 kernel written in Bass

```python
import numpy as np
import jax
import jax.numpy as jnp

def _softmax(x, axis=-1):
    return jax.nn.softmax(x, axis=axis)

def _gelu(x):
    return jax.nn.gelu(x, approximate=True)

def _silu(x):
    return jax.nn.silu(x)

def _sigmoid(x):
    return jax.nn.sigmoid(x)

def _layernorm(x, axis=-1, eps=1e-05):
    m = jnp.mean(x, axis=axis, keepdims=True)
    v = jnp.var(x, axis=axis, keepdims=True)
    return (x - m) / jnp.sqrt(v + eps)

def _scatter_add(tgt, idx, src, axis=0):
    return tgt.at[idx].add(src)

def _segment_sum(src, seg, n):
    return jax.ops.segment_sum(src, seg, n)
kernel_name = 'mk_cond_resid_d2_seqx_r4_c720a4'

def setup_inputs(seed: int=0):
    np.random.seed(seed)
    _w = jnp.asarray

    def _rec_inputs():
        import jax
        import jax.numpy as jnp
        _rk = jax.random.key(seed)
        x = -0.0003929 + 0.9999 * jax.random.normal(jax.random.fold_in(_rk, 1), (8, 256, 256), jnp.float32)
        _lenS = 256 - jax.random.randint(jax.random.fold_in(_rk, 7), (8,), 0, max(1, 256 // 4) + 1, jnp.int32)
        _lenS2 = 256 - jax.random.randint(jax.random.fold_in(_rk, 8), (8,), 0, max(1, 256 // 4) + 1, jnp.int32)
        itok_B_0_7 = jax.random.randint(jax.random.fold_in(_rk, 11), (8,), 0, 8, jnp.int32)
        itok_B_0_15 = jax.random.randint(jax.random.fold_in(_rk, 12), (8,), 0, 16, jnp.int32)
        return (x, itok_B_0_7, itok_B_0_15)
    x, itok_B_0_7, itok_B_0_15 = _rec_inputs()

    def _L0_cond_setup():
        import jax, jax.numpy as jnp
        import numpy as np
        B, S, D, F = (32, 128, 256, 1024)
        R_COMMON, R_DOMAIN, E = (16, 16, 8)
        ALPHA = 2.0

        def _expert_lora(x, expert_ids, Wa, Wb):
            Ab = Wa[expert_ids]
            Bb = Wb[expert_ids]
            low = jnp.einsum('bsd,brd->bsr', x, Ab)
            return ALPHA * jnp.einsum('bsr,bor->bso', low, Bb)
        key = jax.random.key(seed)
        ks = jax.random.split(key, 12)
        sd = lambda k, shape: jax.random.normal(k, shape, dtype=jnp.float32) * (1.0 / np.sqrt(shape[-1]))
        return {'hidden_states': jax.random.normal(ks[0], (B, S, D), dtype=jnp.float32), 'expert_ids': jax.random.randint(ks[1], (B,), 0, E, dtype=jnp.int32), 'wi': sd(ks[2], (F, D)), 'wo': sd(ks[3], (D, F)), 'common_wi_a': sd(ks[4], (R_COMMON, D)), 'common_wi_b': sd(ks[5], (F, R_COMMON)), 'common_wo_a': sd(ks[6], (R_COMMON, F)), 'common_wo_b': sd(ks[7], (D, R_COMMON)), 'experts_wi_a': sd(ks[8], (E, R_DOMAIN, D)), 'experts_wi_b': sd(ks[9], (F, R_DOMAIN)) * jnp.ones((E, 1, 1)) * 0.0 + sd(ks[9], (E, F, R_DOMAIN)), 'experts_wo_a': sd(ks[10], (E, R_DOMAIN, F)), 'experts_wo_b': sd(ks[11], (E, D, R_DOMAIN))}
    _L0_cond_all = _L0_cond_setup()
    _L0_cond_in = {k: v for k, v in _L0_cond_all.items() if k in ('wi', 'wo', 'common_wi_a', 'common_wi_b', 'common_wo_a', 'common_wo_b', 'experts_wi_a', 'experts_wi_b', 'experts_wo_a', 'experts_wo_b')}
    del _L0_cond_all

    def _L1_cond_setup():
        import jax, jax.numpy as jnp
        import numpy as np
        B, N, DIM = (32, 256, 256)
        HID = 1024
        PART = 64
        OUT = 256
        SHARED = OUT - PART
        E = 16
        key = jax.random.key(seed)
        ks = jax.random.split(key, 8)
        s = 0.02
        return {'x': jax.random.normal(ks[0], (B, N, DIM), dtype=jnp.float32), 'indices': jax.random.randint(ks[1], (B,), 0, E, dtype=jnp.int64), 'fc1_w': jax.random.normal(ks[2], (HID, DIM), dtype=jnp.float32) * s, 'fc1_b': jnp.zeros((HID,), dtype=jnp.float32), 'fc2_w': jax.random.normal(ks[3], (SHARED, HID), dtype=jnp.float32) * s, 'fc2_b': jnp.zeros((SHARED,), dtype=jnp.float32), 'experts_w': jax.random.normal(ks[4], (E, PART, HID), dtype=jnp.float32) * s, 'experts_b': jnp.zeros((E, PART), dtype=jnp.float32)}
    _L1_cond_all = _L1_cond_setup()
    _L1_cond_in = {k: v for k, v in _L1_cond_all.items() if k in ('fc1_w', 'fc1_b', 'fc2_w', 'fc2_b', 'experts_w', 'experts_b')}
    del _L1_cond_all
    return {'x': x, 'itok_B_0_7': itok_B_0_7, 'itok_B_0_15': itok_B_0_15, 'L0_cond_wi': _L0_cond_in['wi'], 'L0_cond_wo': _L0_cond_in['wo'], 'L0_cond_common_wi_a': _L0_cond_in['common_wi_a'], 'L0_cond_common_wi_b': _L0_cond_in['common_wi_b'], 'L0_cond_common_wo_a': _L0_cond_in['common_wo_a'], 'L0_cond_common_wo_b': _L0_cond_in['common_wo_b'], 'L0_cond_experts_wi_a': _L0_cond_in['experts_wi_a'], 'L0_cond_experts_wi_b': _L0_cond_in['experts_wi_b'], 'L0_cond_experts_wo_a': _L0_cond_in['experts_wo_a'], 'L0_cond_experts_wo_b': _L0_cond_in['experts_wo_b'], 'L1_cond_fc1_w': _L1_cond_in['fc1_w'], 'L1_cond_fc1_b': _L1_cond_in['fc1_b'], 'L1_cond_fc2_w': _L1_cond_in['fc2_w'], 'L1_cond_fc2_b': _L1_cond_in['fc2_b'], 'L1_cond_experts_w': _L1_cond_in['experts_w'], 'L1_cond_experts_b': _L1_cond_in['experts_b']}

def reference(x, itok_B_0_7, itok_B_0_15, L0_cond_wi, L0_cond_wo, L0_cond_common_wi_a, L0_cond_common_wi_b, L0_cond_common_wo_a, L0_cond_common_wo_b, L0_cond_experts_wi_a, L0_cond_experts_wi_b, L0_cond_experts_wo_a, L0_cond_experts_wo_b, L1_cond_fc1_w, L1_cond_fc1_b, L1_cond_fc2_w, L1_cond_fc2_b, L1_cond_experts_w, L1_cond_experts_b):
    import jax
    import jax.numpy as jnp

    def _L0_cond_ref(hidden_states, expert_ids, wi, wo, common_wi_a, common_wi_b, common_wo_a, common_wo_b, experts_wi_a, experts_wi_b, experts_wo_a, experts_wo_b):
        import jax, jax.numpy as jnp
        import numpy as np
        B, S, D, F = (32, 128, 256, 1024)
        R_COMMON, R_DOMAIN, E = (16, 16, 8)
        ALPHA = 2.0

        def _expert_lora(x, expert_ids, Wa, Wb):
            Ab = Wa[expert_ids]
            Bb = Wb[expert_ids]
            low = jnp.einsum('bsd,brd->bsr', x, Ab)
            return ALPHA * jnp.einsum('bsr,bor->bso', low, Bb)
        x = hidden_states
        hidden_i = jnp.einsum('bsd,fd->bsf', x, wi)
        hidden_i += ALPHA * jnp.einsum('bsr,fr->bsf', jnp.einsum('bsd,rd->bsr', x, common_wi_a), common_wi_b)
        hidden_i += _expert_lora(x, expert_ids, experts_wi_a, experts_wi_b)
        hidden_i = jax.nn.relu(hidden_i)
        hidden_o = jnp.einsum('bsf,df->bsd', hidden_i, wo)
        hidden_o += ALPHA * jnp.einsum('bsr,dr->bsd', jnp.einsum('bsf,rf->bsr', hidden_i, common_wo_a), common_wo_b)
        hidden_o += _expert_lora(hidden_i, expert_ids, experts_wo_a, experts_wo_b)
        return hidden_o

    def _L1_cond_ref(x, indices, fc1_w, fc1_b, fc2_w, fc2_b, experts_w, experts_b):
        import jax, jax.numpy as jnp
        import numpy as np
        B, N, DIM = (32, 256, 256)
        HID = 1024
        PART = 64
        OUT = 256
        SHARED = OUT - PART
        E = 16
        h = jax.nn.gelu(jnp.einsum('bnd,hd->bnh', x, fc1_w) + fc1_b, approximate=False)
        shared = jnp.einsum('bnh,sh->bns', h, fc2_w) + fc2_b
        We = experts_w[indices]
        be = experts_b[indices]
        expert_x = jnp.einsum('bnh,bph->bnp', h, We) + be[:, None, :]
        return jnp.concatenate([shared, expert_x], axis=-1)
    x = x + _L0_cond_ref(x, itok_B_0_7, L0_cond_wi, L0_cond_wo, L0_cond_common_wi_a, L0_cond_common_wi_b, L0_cond_common_wo_a, L0_cond_common_wo_b, L0_cond_experts_wi_a, L0_cond_experts_wi_b, L0_cond_experts_wo_a, L0_cond_experts_wo_b)
    x = x + _L1_cond_ref(x, itok_B_0_15, L1_cond_fc1_w, L1_cond_fc1_b, L1_cond_fc2_w, L1_cond_fc2_b, L1_cond_experts_w, L1_cond_experts_b)
    return x

_drawn_inputs = setup_inputs


def setup_inputs(seed=0):
    import zlib

    import numpy as np

    out = dict(_drawn_inputs(seed))
    spreads = {'L1_cond_fc1_b': (0.0, 0.8),
     'L1_cond_fc2_b': (0.0, 0.651),
     'L1_cond_experts_b': (0.0, 0.8)}
    factors = {}
    for name, (base, spread) in spreads.items():
        noise = np.random.default_rng([zlib.crc32(name.encode()), seed]).standard_normal(out[name].shape)
        drawn = base * np.exp(spread * noise) if base else spread * noise
        out[name] = jnp.asarray(drawn.astype(out[name].dtype))
    for name, factor in factors.items():
        out[name] = (out[name] * factor).astype(out[name].dtype)
    return out
```

```python
from contextlib import ExitStack

import concourse.bass as bass
from concourse import mybir

P = 128
B, T, D = 8, 256, 256
F = 1024
RANK = 32
PART = 64
SHARED = D - PART
ALPHA = 2.0
DC = D // P
FC = F // P
NJ = 4
FJ = FC // NJ
PAIRS = B // 2
T2 = 2 * T
FACW = F + D
F2W = D + P
GROUPS = P // RANK


def program(nc, x, experts_in, fac_common, fac_expert, wi, wo, fc1, fc2, bias1, bias2, idx0, idx1, out):
    f32, f32r, i32 = mybir.dt.float32, mybir.dt.float32r, mybir.dt.int32
    ALU = mybir.AluOpType
    ACT = mybir.ActivationFunctionType

    with ExitStack() as ctx:
        def sb(name, shape, dt=f32):
            return ctx.enter_context(nc.sbuf_tensor(name, shape, dt))

        def pb(name):
            return ctx.enter_context(nc.psum_tensor(name, [P, 512], f32))

        def sem(name):
            return ctx.enter_context(nc.semaphore(name))

        def f(ap):
            return ap.bitcast(f32)

        idx0_sb = sb("idx0_sb", [1, B], i32)
        idx1_sb = sb("idx1_sb", [1, B], i32)
        x_raw = sb("x_raw", [P, 2, DC * T])
        fac_raw = [sb(f"fac{n}_raw", [P, FACW]) for n in (1, 2)]
        wi_raw = sb("wi_raw", [P, NJ, DC * FJ * P])
        wo_raw = sb("wo_raw", [P, NJ, FJ * D])
        fc_raw = sb("fc_raw", [P, FC * D])
        expert_raw = sb("expert_raw", [P, 2, FC * PART + 1])
        bias1_sb = sb("bias1_sb", [P, FC])
        bias2_sb = sb("bias2_sb", [P, 1])
        x_hi, x_lo = (sb(f"x_{s}", [P, 2, DC * T], f32r) for s in ("hi", "lo"))
        fac = [sb(f"fac{n}", [P, FACW], f32r) for n in (1, 2)]
        w1_hi, w1_lo = (sb(f"w1_{s}", [P, NJ, DC * FJ * P], f32r) for s in ("hi", "lo"))
        w2_hi, w2_lo = (sb(f"w2_{s}", [P, NJ, FJ * D], f32r) for s in ("hi", "lo"))
        h_hi, h_lo = (sb(f"h_{s}", [P, NJ, FJ * T], f32r) for s in ("hi", "lo"))
        fc1_hi, fc1_lo = (sb(f"fc1_{s}", [P, FC, D], f32r) for s in ("hi", "lo"))
        fc2_hi, fc2_lo = (sb(f"fc2_{s}", [P, FC, F2W], f32r) for s in ("hi", "lo"))
        x1_hi, x1_lo = (sb(f"x1_{s}", [P, DC, T2], f32r) for s in ("hi", "lo"))
        g_hi, g_lo = (sb(f"g_{s}", [P, FC, T2], f32r) for s in ("hi", "lo"))
        w_sum = sb("w_sum", [P, 2, 512])
        g_full = sb("g_full", [P, 2, T2])
        x1 = sb("x1", [P, DC, T2])
        x1_bias = sb("x1_bias", [P, DC, T2])

        ps_w = pb("ps_w")
        ps_a = [pb("ps_a0"), pb("ps_a1")]
        ps_b = pb("ps_b")
        ps_c = [pb("ps_c0"), pb("ps_c1")]
        ps_d = [pb("ps_d0"), pb("ps_d1")]
        ps_first = [ps_w, ps_c[0], ps_c[1], ps_d[1]]

        in_idx = sem("in_idx")
        in_x = [sem("in_x0"), sem("in_x1")]
        in_fac = [sem("in_fac1"), sem("in_fac2")]
        in_common = sem("in_common")
        in_wi = [sem(f"in_wi{j}") for j in range(NJ)]
        in_wo = sem("in_wo")
        in_fc1 = sem("in_fc1")
        in_fc2 = sem("in_fc2")
        in_expert = sem("in_expert")
        in_bias = sem("in_bias")
        out_stored = sem("out_stored")
        fold1_done = sem("fold1_done")
        fold2_done = sem("fold2_done")
        a_done = sem("a_done")
        b_done = sem("b_done")
        c_done = sem("c_done")
        d_done = sem("d_done")
        fac_rounded = [sem("fac1_rounded"), sem("fac2_rounded")]
        fac_ready = [sem("fac1_ready"), sem("fac2_ready")]
        x_rounded, x_ready = sem("x_rounded"), sem("x_ready")
        w_summed, w_rounded, w_ready = sem("w_summed"), sem("w_rounded"), sem("w_ready")
        h_rounded, h_ready = sem("h_rounded"), sem("h_ready")
        x1_summed, x1_rounded, x1_ready = sem("x1_summed"), sem("x1_rounded"), sem("x1_ready")
        g_made, g_rounded, g_ready = sem("g_made"), sem("g_rounded"), sem("g_ready")
        fc1_rounded, fc1_ready = sem("fc1_rounded"), sem("fc1_ready")
        fc2_rounded, fc2_ready = sem("fc2_rounded"), sem("fc2_ready")
        expert_rounded, expert_ready = sem("expert_rounded"), sem("expert_ready")
        bias_added = sem("bias_added")
        out_made = sem("out_made")

        block = ctx.enter_context(nc.Block())

        @block.sync
        def _(sp):
            def load_factors(n, b, row):
                for g in range(GROUPS):
                    sp.dma_start(fac_raw[n][g * RANK + RANK // 2:(g + 1) * RANK, :],
                                 fac_expert[bass.ds(row, 1), n, :, :].rearrange("a r n -> (a r) n"))\
                        .then_inc(in_fac[n], 16)

            def load_x(b, u):
                sp.dma_start(x_raw[:, u, :], x[bass.ds(b, 1), :, :].rearrange("a p n -> (a p) n"))\
                    .then_inc(in_x[u], 16)

            def load_expert(p, u, row):
                sp.dma_start(expert_raw[:, u, :],
                             experts_in[bass.ds(row, 1), :, :].rearrange("a p n -> (a p) n"))\
                    .then_inc(in_expert, 16)

            def row0(b):
                return sp.value_load(idx0_sb[0:1, bass.ds(b, 1)], min_val=0, max_val=fac_expert.shape[0] - 1)

            def row1(b):
                return sp.value_load(idx1_sb[0:1, bass.ds(b, 1)], min_val=0, max_val=experts_in.shape[0] - 1)

            def step(p, block0=True, block1=True, more=True):
                if block1:
                    rows = [row1(2 * p), row1(2 * p + 1)] if block0 else None
                for u in range(2):
                    b = 2 * p + u
                    if block0 and more:
                        row = row0(b + 2)
                        sp.wait_ge(fac_ready[0], 3 * (b + 2))
                        load_factors(0, b + 2, row)
                    if u == 0 and block1 and block0:
                        sp.wait_ge(expert_ready, 2 * p)
                        sp.wait_ge(bias_added, 3 * p)
                        for v in range(2):
                            load_expert(p, v, rows[v])
                    if block0 and more:
                        sp.wait_ge(fac_ready[1], 3 * (b + 2))
                        load_factors(1, b + 2, row)
                        sp.wait_ge(x1_summed, b + 1)
                        load_x(b + 2, u)

            def store(q):
                sp.wait_ge(out_made, 2 * q + 2)
                sp.dma_start(out[bass.ds(q, 1), :, :].rearrange("a p n -> (a p) n"),
                             x1_bias[:, :, :].rearrange("p c t -> p (c t)")).then_inc(out_stored, 16)

            sp.dma_start(idx0_sb[:, :], idx0).then_inc(in_idx, 16)
            sp.dma_start(idx1_sb[:, :], idx1).then_inc(in_idx, 16)
            for n in range(2):
                for g in range(GROUPS):
                    sp.dma_start(fac_raw[n][g * RANK:g * RANK + RANK // 2, :], fac_common[n, :, :])\
                        .then_inc(in_common, 16)
                if n == 0:
                    sp.wait_ge(in_idx, 32)
                    first = row0(0)
                load_factors(n, 0, first)
                if n == 0:
                    sp.dma_start(wi_raw[:, 0, :], wi[:, 0, :]).then_inc(in_wi[0], 16)
                    load_x(0, 0)
                    for j in range(1, NJ):
                        sp.dma_start(wi_raw[:, j, :], wi[:, j, :]).then_inc(in_wi[j], 16)
            sp.dma_start(wo_raw[:, :, :], wo).then_inc(in_wo, 16)
            second = row0(1)
            sp.wait_ge(fac_ready[0], 3)
            load_factors(0, 1, second)
            load_x(1, 1)
            sp.wait_ge(fac_ready[1], 3)
            load_factors(1, 1, second)
            sp.dma_start(fc_raw[:, :], fc1).then_inc(in_fc1, 16)
            sp.dma_start(bias1_sb[:, :], bias1).then_inc(in_bias, 16)
            sp.dma_start(bias2_sb[:, :], bias2).then_inc(in_bias, 16)
            for u in range(2):
                load_expert(0, u, row1(u))
            sp.wait_ge(fc1_ready, NJ)
            sp.dma_start(fc_raw[:, 0:FC * SHARED], fc2).then_inc(in_fc2, 16)
            step(0, block1=False)
            step(1)
            with sp.Fori(2, PAIRS - 1) as p:
                store(p - 2)
                step(p)
            store(PAIRS - 3)
            step(PAIRS - 1, more=False)
            for q in range(PAIRS - 2, PAIRS):
                store(q)
            sp.wait_ge(out_stored, 16 * PAIRS)

        @block.tensor
        def _(pe):
            def products(acc, w, v, start, stop):
                pe.matmul(acc, w[0], v[0], start=start, stop=False, skip_group_check=True)
                pe.matmul(acc, w[0], v[1], start=False, stop=False, skip_group_check=True)
                return pe.matmul(acc, w[1], v[0], start=False, stop=stop, skip_group_check=True)

            def fold1(b, j, bank=ps_w, first=False):
                if j == 0:
                    pe.wait_ge(fac_ready[0], 3 * (b + 1))
                if bank is ps_w and not (first and j == 0):
                    pe.wait_ge(w_summed, 8 * b + j)
                for c in range(DC):
                    mm = pe.matmul(bank[:, c * FJ * P:(c + 1) * FJ * P], fac[0][:, F + c * P:F + (c + 1) * P],
                                   fac[0][:, j * FJ * P:(j + 1) * FJ * P], start=True, stop=True)
                mm.then_inc(fold1_done, 1)

            def fold2(b, j):
                if j == 0:
                    pe.wait_ge(fac_ready[1], 3 * (b + 1))
                pe.wait_ge(w_summed, 8 * b + NJ + j)
                for i in range(FJ):
                    k = j * FJ + i
                    mm = pe.matmul(ps_w[:, i * D:(i + 1) * D], fac[1][:, k * P:(k + 1) * P],
                                   fac[1][:, F:F + D], start=True, stop=True)
                mm.then_inc(fold2_done, 1)

            def unit_a(b, u, j, first):
                if j == 0:
                    pe.wait_ge(x_ready, b + 1)
                pe.wait_ge(w_ready, 8 * b + j + 1)
                if not first or j >= 2:
                    pe.wait_ge(h_ready, NJ * b + j - 1)
                for i in range(FJ):
                    for c in range(DC):
                        w = slice((c * FJ + i) * P, (c * FJ + i + 1) * P)
                        v = slice(c * T, (c + 1) * T)
                        mm = products(ps_a[j % 2][:, i * T:(i + 1) * T], (w1_hi[:, j, w], w1_lo[:, j, w]),
                                      (x_hi[:, u, v], x_lo[:, u, v]), c == 0, c == DC - 1)
                mm.then_inc(a_done, 1)

            def unit_b(b, j, first):
                if j == 0 and not first:
                    pe.wait_ge(x1_summed, b)
                pe.wait_ge(w_ready, 8 * b + NJ + j + 1)
                pe.wait_ge(h_ready, NJ * b + j + 1)
                for i in range(FJ):
                    for c in range(DC):
                        w = slice(i * D + c * P, i * D + (c + 1) * P)
                        v = slice(i * T, (i + 1) * T)
                        mm = products(ps_b[:, c * T:(c + 1) * T], (w2_hi[:, j, w], w2_lo[:, j, w]),
                                      (h_hi[:, j, v], h_lo[:, j, v]), j == i == c == 0,
                                      j == NJ - 1 and i == FJ - 1)
                mm.then_inc(b_done, 1)

            def unit_c(q, k, first):
                if k == 0:
                    pe.wait_ge(x1_ready, 2 * q + 2)
                    pe.wait_ge(fc1_ready, NJ)
                if not first or k >= 2:
                    pe.wait_ge(g_made, FC * q + k - 1)
                for c in range(DC):
                    w = slice(c * P, (c + 1) * P)
                    mm = products(ps_c[k % 2][:, :], (fc1_hi[:, k, w], fc1_lo[:, k, w]),
                                  (x1_hi[:, c, :], x1_lo[:, c, :]), c == 0, c == DC - 1)
                mm.then_inc(c_done, 1)

            def unit_d(q, k, first):
                if k == 0:
                    pe.wait_ge(expert_ready, 2 * q + 2)
                    pe.wait_ge(fc2_ready, 2)
                    if not first:
                        pe.wait_ge(out_made, 2 * q)
                pe.wait_ge(g_ready, FC * q + k + 1)
                products(ps_d[0][:, :], (fc2_hi[:, k, 0:P], fc2_lo[:, k, 0:P]),
                         (g_hi[:, k, :], g_lo[:, k, :]), k == 0, k == FC - 1)
                for v in range(2):
                    w = slice((1 + v) * P, (2 + v) * P)
                    t = slice(v * T, (v + 1) * T)
                    mm = products(ps_d[1][:, t], (fc2_hi[:, k, w], fc2_lo[:, k, w]),
                                  (g_hi[:, k, t], g_lo[:, k, t]), k == v == 0, k == FC - 1)
                mm.then_inc(d_done, 1)

            def step(p, block0=True, block1=True, first=False, second=False, last=False):
                for s in range(16):
                    u, j = s // 8, s % NJ
                    b = 2 * p + u
                    start = first and u == 0
                    if block0 and s % 8 < NJ:
                        fold2(b, j)
                        unit_a(b, u, j, start)
                    elif block0:
                        if not (last and u == 1):
                            fold1(b + 1, j)
                        unit_b(b, j, start)
                    if block1 and s < FC:
                        unit_c(p - 1, s, second)
                    elif block1:
                        unit_d(p - 1, s - FC, second)

            for j in range(NJ):
                fold1(0, j, ps_first[j], True)
            step(0, block1=False, first=True)
            step(1, second=True)
            with pe.Fori(2, PAIRS - 1) as p:
                step(p)
            step(PAIRS - 1, last=True)
            step(PAIRS, block0=False)

        @block.scalar
        def _(act):
            def round_factors(n, b, first=False):
                act.wait_ge(in_fac[n], 16 * GROUPS * (b + 1))
                if first:
                    act.wait_ge(in_common, 16 * GROUPS * 2)
                else:
                    act.wait_ge(fold1_done if n == 0 else fold2_done, NJ * b)
                act.activation(fac[n][:, :], fac_raw[n][:, :], ACT.Copy).then_inc(fac_rounded[n], 1)

            def round_x(b, u, p, first=False):
                act.wait_ge(in_x[u], 16 * (p + 1))
                if not first:
                    act.wait_ge(a_done, NJ * (b - 1))
                act.activation(x_hi[:, u, :], x_raw[:, u, :], ACT.Copy).then_inc(x_rounded, 1)

            def round_w(n, j, dst, used, used_n):
                act.wait_ge(w_summed, n + 1)
                if used is not None:
                    act.wait_ge(used, used_n)
                act.activation(dst[:, j, :], w_sum[:, j % 2, :], ACT.Copy).then_inc(w_rounded, 1)

            def relu(b, j, first):
                act.wait_ge(a_done, NJ * b + j + 1)
                if not first:
                    act.wait_ge(b_done, NJ * (b - 1) + j + 1)
                act.activation(h_hi[:, j, :], ps_a[j % 2][:, :], ACT.Relu).then_inc(h_rounded, 1)

            def gelu(q, k, first):
                act.wait_ge(c_done, FC * q + k + 1)
                if not first or k >= 2:
                    act.wait_ge(g_ready, FC * q + k - 1)
                act.activation(g_full[:, k % 2, :], ps_c[k % 2][:, :], ACT.Gelu, bias=bias1_sb[:, k:k + 1])\
                    .then_inc(g_made, 1)
                act.wait_ge(g_made, FC * q + k + 1)
                if not first:
                    act.wait_ge(d_done, FC * (q - 1) + k + 1)
                act.activation(g_hi[:, k, :], g_full[:, k % 2, :], ACT.Copy).then_inc(g_rounded, 1)

            def round_x1(b, u, p, first):
                act.wait_ge(x1_summed, b + 1)
                if not first:
                    act.wait_ge(c_done, FC * p)
                t = slice(u * T, (u + 1) * T)
                act.activation(x1_hi[:, :, t], x1[:, :, t], ACT.Copy).then_inc(x1_rounded, 1)

            def round_fc1(j):
                act.wait_ge(in_fc1, 16)
                k = slice(j * FJ, (j + 1) * FJ)
                act.activation(fc1_hi[:, k, :], fc_raw[:, j * FJ * D:(j + 1) * FJ * D]
                               .rearrange("p (k n) -> p k n", k=FJ), ACT.Copy).then_inc(fc1_rounded, 1)

            def round_fc2():
                act.wait_ge(in_fc2, 16)
                raw = fc_raw[:, 0:FC * SHARED].rearrange("p (k n) -> p k n", k=FC)
                act.activation(fc2_hi[:, :, 0:SHARED], raw, ACT.Copy).then_inc(fc2_rounded, 1)
                act.activation(fc2_hi[:, :, D:D + PART], raw[:, :, P:SHARED], ACT.Copy).then_inc(fc2_rounded, 1)

            def step(p, block0=True, block1=True, first=False, second=False, last=False):
                for s in range(16):
                    u, j = s // 8, s % NJ
                    b = 2 * p + u
                    start = first and u == 0
                    if block0 and s % 8 < NJ:
                        round_w(8 * b + NJ + j, j, w2_hi, None if start else b_done, NJ * (b - 1) + j + 1)
                        relu(b, j, start)
                        if j == 1 and not (last and u == 1):
                            round_factors(0, b + 1)
                    elif block0:
                        if not (last and u == 1):
                            round_w(8 * b + 8 + j, j, w1_hi, a_done, NJ * b + j + 1)
                            if j == 1:
                                round_factors(1, b + 1)
                            if j == 2:
                                round_x(b + 1, 1 - u, p + u, start)
                    if block1 and s < FC:
                        if s == 0 and second:
                            act.wait_ge(in_bias, 32)
                        gelu(p - 1, s, second)
                    if block0 and s == 8:
                        round_x1(b - 1, 0, p, first)
                    if block0 and s == 15:
                        round_x1(b, 1, p, first)
                    if first and 4 <= s < 8:
                        round_fc1(j)
                    if first and s == 12:
                        round_fc2()

            round_factors(0, 0, True)
            round_x(0, 0, 0, True)
            for j in range(NJ):
                round_w(j, j, w1_hi, None, 0)
            round_factors(1, 0, True)
            step(0, block1=False, first=True)
            step(1, second=True)
            with act.Fori(2, PAIRS - 1) as p:
                step(p)
            step(PAIRS - 1, last=True)
            step(PAIRS, block0=False)

        def split_factors(eng, n, b, in_turn=False):
            eng.wait_ge(fac_rounded[n], b + 1)
            for i, (rows, cols) in enumerate(((slice(2 * RANK, P), slice(0, F)),
                                              (slice(RANK, 2 * RANK), slice(F, FACW)),
                                              (slice(3 * RANK, P), slice(F, FACW)))):
                if i and in_turn:
                    eng.wait_ge(fac_ready[n], 3 * b + i)
                eng.tensor_tensor(fac[n][rows, cols], fac_raw[n][rows, cols], f(fac[n][rows, cols]),
                                  ALU.subtract).then_inc(fac_ready[n], 1)

        def split_x(eng, b, u):
            eng.wait_ge(x_rounded, b + 1)
            eng.tensor_tensor(x_lo[:, u, :], x_raw[:, u, :], f(x_hi[:, u, :]), ALU.subtract)\
                .then_inc(x_ready, 1)

        @block.vector
        def _(dve):
            def sum_w(n, j, done, done_n, raw, bank=ps_w, first=False):
                dve.wait_ge(done, done_n)
                if not first or j >= 2:
                    dve.wait_ge(w_ready, n - 1)
                dve.scalar_tensor_tensor(out=w_sum[:, j % 2, :], in0=bank[:, :], scalar=ALPHA, in1=raw[:, j, :],
                                         op0=ALU.mult, op1=ALU.add).then_inc(w_summed, 1)

            def lo_w(n, j, hi, lo):
                dve.wait_ge(w_rounded, n + 1)
                dve.tensor_tensor(lo[:, j, :], w_sum[:, j % 2, :], f(hi[:, j, :]), ALU.subtract)\
                    .then_inc(w_ready, 1)

            def lo_h(b, j):
                dve.wait_ge(h_rounded, NJ * b + j + 1)
                dve.scalar_tensor_tensor(out=h_lo[:, j, :], in0=ps_a[j % 2][:, :], scalar=0.0,
                                         in1=f(h_hi[:, j, :]), op0=ALU.max, op1=ALU.subtract)\
                    .then_inc(h_ready, 1)

            def lo_g(q, k):
                dve.wait_ge(g_rounded, FC * q + k + 1)
                dve.tensor_tensor(g_lo[:, k, :], g_full[:, k % 2, :], f(g_hi[:, k, :]), ALU.subtract)\
                    .then_inc(g_ready, 1)

            def sum_x1(b, u, p, first):
                dve.wait_ge(b_done, NJ * (b + 1))
                if not first:
                    dve.wait_ge(bias_added, 3 * p)
                dve.tensor_tensor(x1[:, :, u * T:(u + 1) * T], ps_b[:, :].rearrange("p (c t) -> p c t", c=DC),
                                  x_raw[:, u, :].rearrange("p (c t) -> p c t", c=DC), ALU.add)\
                    .then_inc(x1_summed, 1)

            def lo_x1(b, u):
                dve.wait_ge(x1_rounded, b + 1)
                t = slice(u * T, (u + 1) * T)
                dve.tensor_tensor(x1_lo[:, :, t], x1[:, :, t], f(x1_hi[:, :, t]), ALU.subtract)\
                    .then_inc(x1_ready, 1)

            def make_out(q):
                dve.wait_ge(d_done, FC * (q + 1))
                dve.wait_ge(bias_added, 3 * (q + 1))
                for c in range(DC):
                    dve.tensor_tensor(x1_bias[:, c, :], ps_d[c][:, :], x1_bias[:, c, :], ALU.add)\
                        .then_inc(out_made, 1)

            def lo_fc1(j):
                dve.wait_ge(fc1_rounded, j + 1)
                k = slice(j * FJ, (j + 1) * FJ)
                dve.tensor_tensor(fc1_lo[:, k, :], fc_raw[:, j * FJ * D:(j + 1) * FJ * D]
                                  .rearrange("p (k n) -> p k n", k=FJ), f(fc1_hi[:, k, :]), ALU.subtract)\
                    .then_inc(fc1_ready, 1)

            def lo_fc2():
                dve.wait_ge(fc2_rounded, 2)
                raw = fc_raw[:, 0:FC * SHARED].rearrange("p (k n) -> p k n", k=FC)
                dve.tensor_tensor(fc2_lo[:, :, 0:SHARED], raw, f(fc2_hi[:, :, 0:SHARED]), ALU.subtract)\
                    .then_inc(fc2_ready, 1)
                dve.tensor_tensor(fc2_lo[:, :, D:D + PART], raw[:, :, P:SHARED], f(fc2_hi[:, :, D:D + PART]),
                                  ALU.subtract).then_inc(fc2_ready, 1)

            def step(p, block0=True, block1=True, first=False, second=False, last=False):
                for s in range(16):
                    u, j = s // 8, s % NJ
                    b = 2 * p + u
                    if block0 and s % 8 < NJ:
                        if first and s == 0:
                            dve.wait_ge(in_wo, 16)
                        sum_w(8 * b + NJ + j, j, fold2_done, NJ * b + j + 1, wo_raw)
                    elif block0 and not (last and u == 1):
                        sum_w(8 * b + 8 + j, j, fold1_done, NJ * (b + 1) + j + 1, wi_raw)
                    if s == 0 and not first and not second:
                        make_out(p - 2)
                    if block1 and 1 <= s <= FC:
                        lo_g(p - 1, s - 1)
                    if block0 and s % 8 < NJ:
                        lo_h(b, j)
                        if s == 8:
                            sum_x1(b - 1, 0, p, first)
                        lo_w(8 * b + NJ + j, j, w2_hi, w2_lo)
                        if s == 8:
                            lo_x1(b - 1, 0)
                    elif block0:
                        if s == 15:
                            sum_x1(b, 1, p, first)
                        if not (last and u == 1):
                            lo_w(8 * b + 8 + j, j, w1_hi, w1_lo)
                        if s == 15:
                            lo_x1(b, 1)
                    if first and 4 <= s < 8:
                        lo_fc1(j)
                    if first and s == 12:
                        lo_fc2()

            split_factors(dve, 0, 0)
            split_x(dve, 0, 0)
            for j in range(NJ):
                dve.wait_ge(in_wi[j], 16)
                sum_w(j, j, fold1_done, j + 1, wi_raw, ps_first[j], True)
                lo_w(j, j, w1_hi, w1_lo)
            split_factors(dve, 1, 0)
            step(0, block1=False, first=True)
            step(1, second=True)
            with dve.Fori(2, PAIRS - 1) as p:
                step(p)
            step(PAIRS - 1, last=True)
            step(PAIRS, block0=False)
            make_out(PAIRS - 1)

        @block.gpsimd
        def _(pool):
            def split_expert(q, first):
                pool.wait_ge(in_expert, 32 * (q + 1))
                if not first:
                    pool.wait_ge(d_done, FC * q)
                def cols(t, v):
                    return t[:, :, (1 + v) * P + PART:(2 + v) * P]
                for v in range(2):
                    raw = expert_raw[:, v, 0:FC * PART].rearrange("p (k n) -> p k n", k=FC)
                    pool.tensor_copy(cols(fc2_hi, v), raw).then_inc(expert_rounded, 1)
                    pool.wait_ge(expert_rounded, 2 * q + 1 + v)
                    pool.tensor_tensor(cols(fc2_lo, v), raw, f(cols(fc2_hi, v)), ALU.subtract)\
                        .then_inc(expert_ready, 1)
                    pool.wait_ge(expert_ready, 2 * q + 1 + v)

            def add_bias(q, first):
                pool.wait_ge(x1_summed, 2 * q + 2)
                if first:
                    pool.wait_ge(in_bias, 32)
                else:
                    pool.wait_ge(out_stored, 16 * q)
                pool.tensor_scalar(x1_bias[:, 0, :], x1[:, 0, :], bias2_sb[:, 0:1], 1.0, ALU.add, ALU.mult)\
                    .then_inc(bias_added, 1)
                pool.wait_ge(bias_added, 3 * q + 1)
                for v in range(2):
                    t = slice(v * T, (v + 1) * T)
                    pool.tensor_scalar(x1_bias[:, 1, t], x1[:, 1, t], expert_raw[:, v, FC * PART:FC * PART + 1],
                                       1.0, ALU.add, ALU.mult).then_inc(bias_added, 1)
                    pool.wait_ge(bias_added, 3 * q + 2 + v)

            def step(p, block0=True, block1=True, first=False, second=False, last=False):
                for u in range(2):
                    b = 2 * p + u
                    more = block0 and not (last and u == 1)
                    if more:
                        split_factors(pool, 0, b + 1, True)
                        pool.wait_ge(fac_ready[0], 3 * (b + 2))
                    if block1 and u == 0:
                        split_expert(p - 1, second)
                        add_bias(p - 1, second)
                    if more:
                        split_factors(pool, 1, b + 1, True)
                        pool.wait_ge(fac_ready[1], 3 * (b + 2))
                        split_x(pool, b + 1, 1 - u)
                        pool.wait_ge(x_ready, b + 2)

            step(0, block1=False, first=True)
            step(1, second=True)
            with pool.Fori(2, PAIRS - 1) as p:
                step(p)
            step(PAIRS - 1, last=True)
            step(PAIRS, block0=False)


def kernel(**inputs):
    import numpy as np
    import concourse.bacc as bacc
    from concourse.bass_utils import run_bass_kernel_spmd

    def get(name):
        return np.asarray(inputs[name])

    x = get("x").reshape(B, T, DC, P).transpose(0, 3, 2, 1).reshape(B, P, DC * T)
    wi = get("L0_cond_wi").reshape(NJ, FJ * P, DC, P).transpose(3, 0, 2, 1).reshape(P, NJ, DC * FJ * P)
    wo = get("L0_cond_wo").reshape(D, NJ, FJ, P).transpose(3, 1, 2, 0).reshape(P, NJ, FJ * D)
    fc1 = get("L1_cond_fc1_w").reshape(FC, P, DC, P).transpose(3, 0, 2, 1).reshape(P, FC * D)
    fc2 = get("L1_cond_fc2_w").reshape(SHARED, FC, P).transpose(2, 1, 0).reshape(P, FC * SHARED)
    common = np.stack([
        np.concatenate([get("L0_cond_common_wi_b").T, get("L0_cond_common_wi_a")], axis=1),
        np.concatenate([get("L0_cond_common_wo_a"), get("L0_cond_common_wo_b").T], axis=1)])
    expert = np.stack([
        np.concatenate([get("L0_cond_experts_wi_b").transpose(0, 2, 1), get("L0_cond_experts_wi_a")], axis=2),
        np.concatenate([get("L0_cond_experts_wo_a"), get("L0_cond_experts_wo_b").transpose(0, 2, 1)], axis=2)],
        axis=1)
    ew = get("L1_cond_experts_w")
    n_experts = ew.shape[0]
    ew = ew.reshape(n_experts, PART, FC, P).transpose(0, 3, 2, 1).reshape(n_experts, P, FC * PART)
    b2 = get("L1_cond_fc2_b")
    bias = np.concatenate([np.broadcast_to(b2[P:], (n_experts, SHARED - P)), get("L1_cond_experts_b")], axis=1)
    ew = np.concatenate([ew, bias[:, :, None]], axis=2)

    arrays = {
        "x": x, "experts_in": ew, "fac_common": common, "fac_expert": expert, "wi": wi, "wo": wo,
        "fc1": fc1, "fc2": fc2, "bias1": get("L1_cond_fc1_b").reshape(FC, P).T, "bias2": b2[:P].reshape(P, 1),
        "idx0": get("itok_B_0_7").reshape(1, B), "idx1": get("itok_B_0_15").reshape(1, B),
    }
    nc = bacc.Bacc("TRN2", target_bir_lowering=False, num_devices=1)
    feeds, args = {}, []
    for name, a in arrays.items():
        a = np.ascontiguousarray(a)
        feeds[f"{name}_dram"] = a
        args.append(nc.dram_tensor(f"{name}_dram", a.shape, mybir.dt.from_np(a.dtype), kind="ExternalInput").ap())
    args.append(nc.dram_tensor("out_dram", (PAIRS, P, DC * T2), mybir.dt.float32, kind="ExternalOutput").ap())
    program(nc, *args)
    r = run_bass_kernel_spmd(nc, [feeds], core_ids=[0])
    got = np.asarray(r.results[0]["out_dram"]).reshape(PAIRS, P, DC, 2, T)
    return got.transpose(0, 3, 4, 2, 1).reshape(B, T, D)
```

```python
from contextlib import ExitStack

import concourse.bass as bass
from concourse import mybir

P = 128
B, T, D = 8, 256, 256
F = 1024
RANK = 32
PART = 64
SHARED = D - PART
ALPHA = 2.0
DC = D // P
FC = F // P
NJ = 4
FJ = FC // NJ
PAIRS = B // 2
T2 = 2 * T
FACW = F + D
F2W = D + P
GROUPS = P // RANK
FIRST = D + FJ * P


def program(nc, x, experts_in, factors, wi, wo, fc1, fc2, bias1, bias2, idx, out):
    f32, f32r, i32 = mybir.dt.float32, mybir.dt.float32r, mybir.dt.int32
    ALU = mybir.AluOpType
    ACT = mybir.ActivationFunctionType

    with ExitStack() as ctx:
        def sb(name, shape, dt=f32):
            return ctx.enter_context(nc.sbuf_tensor(name, shape, dt))

        def pb(name):
            return ctx.enter_context(nc.psum_tensor(name, [P, 512], f32))

        def sem(name):
            return ctx.enter_context(nc.semaphore(name))

        def f(ap):
            return ap.bitcast(f32)

        idx_sb = sb("idx_sb", [1, 2 * B], i32)
        x_raw = sb("x_raw", [P, 2, DC * T])
        fac_raw = [sb(f"fac{n}_raw", [P, FACW]) for n in (1, 2)]
        wi_raw = sb("wi_raw", [P, NJ, DC * FJ * P])
        wo_raw = sb("wo_raw", [P, NJ, FJ * D])
        fc_raw = sb("fc_raw", [P, FC * D])
        expert_raw = sb("expert_raw", [P, 2, FC * PART + 1])
        bias1_sb = sb("bias1_sb", [P, FC])
        bias2_sb = sb("bias2_sb", [P, 1])
        x_hi, x_lo = (sb(f"x_{s}", [P, 2, DC * T], f32r) for s in ("hi", "lo"))
        fac = [sb(f"fac{n}", [P, FACW], f32r) for n in (1, 2)]
        w1_hi, w1_lo = (sb(f"w1_{s}", [P, NJ, DC * FJ * P], f32r) for s in ("hi", "lo"))
        w2_hi, w2_lo = (sb(f"w2_{s}", [P, NJ, FJ * D], f32r) for s in ("hi", "lo"))
        h_hi, h_lo = (sb(f"h_{s}", [P, NJ, FJ * T], f32r) for s in ("hi", "lo"))
        fc1_hi, fc1_lo = (sb(f"fc1_{s}", [P, FC, D], f32r) for s in ("hi", "lo"))
        fc2_hi, fc2_lo = (sb(f"fc2_{s}", [P, FC, F2W], f32r) for s in ("hi", "lo"))
        x1_hi, x1_lo = (sb(f"x1_{s}", [P, DC, T2], f32r) for s in ("hi", "lo"))
        g_hi, g_lo = (sb(f"g_{s}", [P, FC, T2], f32r) for s in ("hi", "lo"))
        zero = sb("zero", [P, 2])
        w_sum = sb("w_sum", [P, 2, 512])
        g_full = sb("g_full", [P, 2, T2])
        x1 = sb("x1", [P, DC, T2])
        x1_bias = sb("x1_bias", [P, DC, T2])

        ps_w = pb("ps_w")
        ps_a = [pb("ps_a0"), pb("ps_a1")]
        ps_b = pb("ps_b")
        ps_c = [pb("ps_c0"), pb("ps_c1")]
        ps_d = [pb("ps_d0"), pb("ps_d1")]
        ps_first = [ps_w, ps_c[0], ps_c[1], ps_d[1]]

        in_idx = sem("in_idx")
        zeroed = sem("zeroed")
        in_x = [sem("in_x0"), sem("in_x1")]
        in_fac = [sem("in_fac1"), sem("in_fac2")]
        in_wi = [sem(f"in_wi{j}") for j in range(NJ)]
        in_wo = sem("in_wo")
        in_fc1 = sem("in_fc1")
        in_fc2 = sem("in_fc2")
        in_expert = sem("in_expert")
        in_bias = sem("in_bias")
        out_stored = sem("out_stored")
        fold1_done = sem("fold1_done")
        fold2_done = sem("fold2_done")
        a_done = sem("a_done")
        b_done = sem("b_done")
        c_done = sem("c_done")
        d_done = sem("d_done")
        fac_rounded = [sem("fac1_rounded"), sem("fac2_rounded")]
        first_ready = sem("first_ready")
        fac_ready = [sem("fac1_ready"), sem("fac2_ready")]
        x_rounded, x_ready = sem("x_rounded"), sem("x_ready")
        w_summed, w_rounded, w_ready = sem("w_summed"), sem("w_rounded"), sem("w_ready")
        h_rounded, h_ready = sem("h_rounded"), sem("h_ready")
        x1_summed, x1_rounded, x1_ready = sem("x1_summed"), sem("x1_rounded"), sem("x1_ready")
        g_made, g_rounded, g_ready = sem("g_made"), sem("g_rounded"), sem("g_ready")
        fc1_rounded, fc1_ready = sem("fc1_rounded"), sem("fc1_ready")
        fc2_rounded, fc2_ready = sem("fc2_rounded"), sem("fc2_ready")
        expert_rounded, expert_ready = sem("expert_rounded"), sem("expert_ready")
        bias_added = sem("bias_added")
        out_made = sem("out_made")

        def expert_cols(t, v):
            return t[:, :, (1 + v) * P + PART:(2 + v) * P]

        block = ctx.enter_context(nc.Block())

        @block.sync
        def _(sp):
            def load_factors(n, row, first=False):
                skip = 0 if first else RANK // 2
                for g in range(GROUPS):
                    sp.dma_start(fac_raw[n][g * RANK + skip:(g + 1) * RANK, :],
                                 factors[bass.ds(row, 1), n, skip:RANK, :].rearrange("a r n -> (a r) n"))\
                        .then_inc(in_fac[n], 16)

            def load_x(b, u):
                sp.dma_start(x_raw[:, u, :], x[bass.ds(b, 1), :, :].rearrange("a p n -> (a p) n"))\
                    .then_inc(in_x[u], 16)

            def load_expert(p, u, row):
                sp.dma_start(expert_raw[:, u, :],
                             experts_in[bass.ds(row, 1), :, :].rearrange("a p n -> (a p) n"))\
                    .then_inc(in_expert, 16)

            def row0(b):
                return sp.value_load(idx_sb[0:1, bass.ds(b, 1)], min_val=0, max_val=factors.shape[0] - 1)

            def row1(b):
                return sp.value_load(idx_sb[0:1, bass.ds(b + B, 1)], min_val=0, max_val=experts_in.shape[0] - 1)

            def store(q):
                for c in range(DC):
                    sp.wait_ge(out_made, DC * q + c + 1)
                    sp.dma_start(out[bass.ds(q, 1), :, c * T2:(c + 1) * T2].rearrange("a p n -> (a p) n"),
                                 x1_bias[:, c, :]).then_inc(out_stored, 16)

            def step(p, block1=True, last=False):
                for u in range(2):
                    b = 2 * p + u
                    if not last:
                        row = row0(b + 2)
                        sp.wait_ge(fac_ready[0], 3 * (b + 2))
                        load_factors(0, row)
                    if u == 0 and block1:
                        rows = [row1(2 * p + v) for v in range(2)]
                        sp.wait_ge(expert_ready, 2 * p)
                        sp.wait_ge(bias_added, 2 * p)
                        for v in range(2):
                            load_expert(p, v, rows[v])
                    if not last:
                        sp.wait_ge(fac_ready[1], 3 * (b + 2))
                        load_factors(1, row)
                        sp.wait_ge(x1_summed, b + 1)
                        load_x(b + 2, u)
                    if u == 0 and not block1:
                        sp.wait_ge(fc1_ready, NJ)
                        sp.dma_start(fc_raw[:, 0:FC * SHARED], fc2).then_inc(in_fc2, 16)
                if block1:
                    store(p - 1)

            sp.dma_start(idx_sb[:, :], idx).then_inc(in_idx, 16)
            sp.wait_ge(in_idx, 16)
            row = row0(0)
            load_factors(0, row, first=True)
            load_factors(1, row, first=True)
            sp.dma_start(wo_raw[:, :, :], wo).then_inc(in_wo, 16)
            row = row0(1)
            sp.wait_ge(fac_ready[0], 3)
            load_factors(0, row)
            load_x(1, 1)
            sp.wait_ge(fac_ready[1], 3)
            load_factors(1, row)
            sp.dma_start(fc_raw[:, :], fc1).then_inc(in_fc1, 16)
            sp.dma_start(bias1_sb[:, :], bias1).then_inc(in_bias, 16)
            sp.dma_start(bias2_sb[:, :], bias2).then_inc(in_bias, 16)
            for u in range(2):
                load_expert(0, u, row1(u))
            step(0, block1=False)
            with sp.Fori(1, PAIRS - 1) as p:
                step(p)
            step(PAIRS - 1, last=True)
            store(PAIRS - 1)
            sp.wait_ge(out_stored, 32 * (PAIRS + 1))

        @block.tensor
        def _(pe):
            def products(acc, w, v, start, stop):
                pe.matmul(acc, w[0], v[0], start=start, stop=False, skip_group_check=True)
                pe.matmul(acc, w[0], v[1], start=False, stop=False, skip_group_check=True)
                return pe.matmul(acc, w[1], v[0], start=False, stop=stop, skip_group_check=True)

            def fold1(b, j, bank=None):
                if bank is ps_first[0]:
                    pe.wait_ge(first_ready, 3)
                elif j == 0 or bank is ps_first[1]:
                    pe.wait_ge(fac_ready[0], 3 * (b + 1))
                if bank is None:
                    bank = ps_w
                    pe.wait_ge(w_summed, 8 * b + j)
                v = slice(D + j * FJ * P, D + (j + 1) * FJ * P)
                for c in range(DC):
                    mm = pe.matmul(bank[:, c * FJ * P:(c + 1) * FJ * P], fac[0][:, c * P:(c + 1) * P],
                                   fac[0][:, v], start=True, stop=True)
                mm.then_inc(fold1_done, 1)

            def fold2(b, j):
                if j == 0:
                    pe.wait_ge(fac_ready[1], 3 * (b + 1))
                pe.wait_ge(w_summed, 8 * b + NJ + j)
                for i in range(FJ):
                    k = j * FJ + i
                    mm = pe.matmul(ps_w[:, i * D:(i + 1) * D], fac[1][:, D + k * P:D + (k + 1) * P],
                                   fac[1][:, 0:D], start=True, stop=True)
                mm.then_inc(fold2_done, 1)

            def unit_a(b, u, j):
                if j == 0:
                    pe.wait_ge(x_ready, b + 1)
                pe.wait_ge(w_ready, 8 * b + j + 1)
                if j >= 2:
                    pe.wait_ge(h_ready, NJ * b + j - 1)
                for i in range(FJ):
                    for c in range(DC):
                        w = slice((c * FJ + i) * P, (c * FJ + i + 1) * P)
                        v = slice(c * T, (c + 1) * T)
                        mm = products(ps_a[j % 2][:, i * T:(i + 1) * T], (w1_hi[:, j, w], w1_lo[:, j, w]),
                                      (x_hi[:, u, v], x_lo[:, u, v]), c == 0, c == DC - 1)
                mm.then_inc(a_done, 1)

            def unit_b(b, j, first):
                if j == 0 and not first:
                    pe.wait_ge(x1_summed, b)
                pe.wait_ge(w_ready, 8 * b + NJ + j + 1)
                pe.wait_ge(h_ready, NJ * b + j + 1)
                for i in range(FJ):
                    for c in range(DC):
                        w = slice(i * D + c * P, i * D + (c + 1) * P)
                        v = slice(i * T, (i + 1) * T)
                        mm = products(ps_b[:, c * T:(c + 1) * T], (w2_hi[:, j, w], w2_lo[:, j, w]),
                                      (h_hi[:, j, v], h_lo[:, j, v]), j == i == c == 0,
                                      j == NJ - 1 and i == FJ - 1)
                mm.then_inc(b_done, 1)

            def unit_c(q, k):
                if k == 0:
                    pe.wait_ge(x1_ready, 2 * q + 2)
                    pe.wait_ge(fc1_ready, NJ)
                if k >= 2:
                    pe.wait_ge(g_made, FC * q + k - 1)
                for c in range(DC):
                    w = slice(c * P, (c + 1) * P)
                    mm = products(ps_c[k % 2][:, :], (fc1_hi[:, k, w], fc1_lo[:, k, w]),
                                  (x1_hi[:, c, :], x1_lo[:, c, :]), c == 0, c == DC - 1)
                mm.then_inc(c_done, 1)

            def unit_d(q, k):
                if k == 0:
                    pe.wait_ge(expert_ready, 2 * q + 2)
                    pe.wait_ge(fc2_ready, 2)
                pe.wait_ge(g_ready, FC * q + k + 1)
                mm = products(ps_d[0][:, :], (fc2_hi[:, k, 0:P], fc2_lo[:, k, 0:P]),
                              (g_hi[:, k, :], g_lo[:, k, :]), k == 0, k == FC - 1)
                mm.then_inc(d_done, 1)
                for v in range(2):
                    w = slice((1 + v) * P, (2 + v) * P)
                    t = slice(v * T, (v + 1) * T)
                    mm = products(ps_d[1][:, t], (fc2_hi[:, k, w], fc2_lo[:, k, w]),
                                  (g_hi[:, k, t], g_lo[:, k, t]), k == v == 0, k == FC - 1)
                mm.then_inc(d_done, 1)

            def step(p, block0=True, block1=True, first=False, last=False):
                for s in range(16):
                    u, j = s // 8, s % NJ
                    b = 2 * p + u
                    if first and s < NJ:
                        unit_a(b, u, j)
                        fold2(b, j)
                    elif block0 and s % 8 < NJ:
                        fold2(b, j)
                        unit_a(b, u, j)
                    elif block0:
                        if not (last and u == 1):
                            fold1(b + 1, j)
                        unit_b(b, j, first and u == 0)
                    if block1 and s < FC:
                        unit_c(p - 1, s)
                    elif block1 and last and s == 14:
                        continue
                    elif block1:
                        if last and s == 15:
                            unit_d(p - 1, 6)
                        unit_d(p - 1, s - FC)

            for j in range(NJ):
                fold1(0, j, ps_first[j])
            step(0, block1=False, first=True)
            with pe.Fori(1, PAIRS - 1) as p:
                step(p)
            step(PAIRS - 1, last=True)
            step(PAIRS, block0=False)

        @block.scalar
        def _(act):
            def round_factors(n, b, first=False, cols=slice(0, FACW)):
                act.wait_ge(in_fac[n], 16 * GROUPS * (b + 1))
                if not first:
                    act.wait_ge(fold1_done if n == 0 else fold2_done, NJ * b)
                act.activation(fac[n][:, cols], fac_raw[n][:, cols], ACT.Copy).then_inc(fac_rounded[n], 1)

            def round_x(b, u, p, first=False):
                act.wait_ge(in_x[u], 16 * (p + 1))
                if not first:
                    act.wait_ge(a_done, NJ * (b - 1))
                act.activation(x_hi[:, u, :], x_raw[:, u, :], ACT.Copy).then_inc(x_rounded, 1)

            def round_w(n, j, dst):
                act.wait_ge(w_summed, n + 1)
                act.activation(dst[:, j, :], w_sum[:, j % 2, :], ACT.Copy).then_inc(w_rounded, 1)

            def relu(b, j):
                act.wait_ge(a_done, NJ * b + j + 1)
                act.activation(h_hi[:, j, :], ps_a[j % 2][:, :], ACT.Relu).then_inc(h_rounded, 1)

            def gelu(q, k):
                act.wait_ge(c_done, FC * q + k + 1)
                if k >= 2:
                    act.wait_ge(g_ready, FC * q + k - 1)
                act.activation(g_full[:, k % 2, :], ps_c[k % 2][:, :], ACT.Gelu, bias=bias1_sb[:, k:k + 1])\
                    .then_inc(g_made, 1)
                act.wait_ge(g_made, FC * q + k + 1)
                act.activation(g_hi[:, k, :], g_full[:, k % 2, :], ACT.Copy).then_inc(g_rounded, 1)

            def round_expert(q):
                act.wait_ge(in_expert, 32 * (q + 1))
                for v in range(2):
                    raw = expert_raw[:, v, 0:FC * PART].rearrange("p (k n) -> p k n", k=FC)
                    act.activation(expert_cols(fc2_hi, v), raw, ACT.Copy).then_inc(expert_rounded, 1)

            def add_bias(q):
                act.wait_ge(x1_summed, 2 * q + 2)
                act.wait_ge(out_stored, 32 * (q + 1))
                act.activation(x1_bias[:, 0, :], x1[:, 0, :], ACT.Identity, bias=bias2_sb[:, 0:1])\
                    .then_inc(bias_added, 1)
                for v in range(2):
                    t = slice(v * T, (v + 1) * T)
                    op = act.activation(x1_bias[:, 1, t], x1[:, 1, t], ACT.Identity,
                                        bias=expert_raw[:, v, FC * PART:FC * PART + 1])
                op.then_inc(bias_added, 1)

            def round_x1(b, u, p, first):
                act.wait_ge(x1_summed, b + 1)
                if not first:
                    act.wait_ge(c_done, FC * p)
                t = slice(u * T, (u + 1) * T)
                act.activation(x1_hi[:, :, t], x1[:, :, t], ACT.Copy).then_inc(x1_rounded, 1)

            def round_fc1(j):
                act.wait_ge(in_fc1, 16)
                k = slice(j * FJ, (j + 1) * FJ)
                act.activation(fc1_hi[:, k, :], fc_raw[:, j * FJ * D:(j + 1) * FJ * D]
                               .rearrange("p (k n) -> p k n", k=FJ), ACT.Copy).then_inc(fc1_rounded, 1)

            def round_fc2():
                act.wait_ge(in_fc2, 16)
                raw = fc_raw[:, 0:FC * SHARED].rearrange("p (k n) -> p k n", k=FC)
                act.activation(fc2_hi[:, :, 0:SHARED], raw, ACT.Copy).then_inc(fc2_rounded, 1)
                act.activation(fc2_hi[:, :, D:D + PART], raw[:, :, P:SHARED], ACT.Copy).then_inc(fc2_rounded, 1)

            def step(p, block0=True, block1=True, first=False, last=False):
                for s in range(16):
                    u, j = s // 8, s % NJ
                    b = 2 * p + u
                    more = block0 and not (last and u == 1)
                    if block1 and 1 <= s <= FC:
                        gelu(p - 1, s - 1)
                    if block1 and s == 2:
                        round_expert(p - 1)
                    if block1 and s == 5:
                        add_bias(p - 1)
                    if block0 and s == 8:
                        round_x1(b - 1, 0, p, first)
                    if first and s < NJ:
                        relu(b, j)
                        round_w(8 * b + NJ + j, j, w2_hi)
                    elif block0 and s % 8 < NJ:
                        round_w(8 * b + NJ + j, j, w2_hi)
                        relu(b, j)
                    elif more:
                        round_w(8 * b + 8 + j, j, w1_hi)
                    if block0 and s == 15:
                        round_x1(b, 1, p, first)
                    if more and s % 8 == 1:
                        round_factors(0, b + 1)
                    if more and s % 8 == 3:
                        round_x(b + 1, 1 - u, p + u, first and u == 0)
                    if more and s % 8 == 5:
                        round_factors(1, b + 1)
                    if first and 4 <= s < 8:
                        round_fc1(j)
                    if first and s == 12:
                        round_fc2()

            act.nop().then_inc(out_stored, 32)
            act.dma_start(x_raw[:, 0, :], x[0, :, :]).then_inc(in_x[0], 16)
            for j in range(NJ):
                act.dma_start(wi_raw[:, j, :], wi[:, j, :]).then_inc(in_wi[j], 16)
            act.wait_ge(zeroed, 1)
            act.activation(zero[:, 1:2], zero[:, 0:1], ACT.Gelu).then_inc(zeroed, 1)
            round_factors(0, 0, True, slice(0, FIRST))
            round_factors(0, 0, True, slice(FIRST, FACW))
            round_x(0, 0, 0, True)
            round_w(0, 0, w1_hi)
            round_w(1, 1, w1_hi)
            round_factors(1, 0, True)
            round_w(2, 2, w1_hi)
            round_w(3, 3, w1_hi)
            step(0, block1=False, first=True)
            act.wait_ge(in_bias, 32)
            with act.Fori(1, PAIRS - 1) as p:
                step(p)
            step(PAIRS - 1, last=True)
            step(PAIRS, block0=False)

        LO_PARTS = ((slice(RANK, 2 * RANK), slice(0, D)), (slice(3 * RANK, P), slice(0, D)),
                    (slice(2 * RANK, P), slice(D, FACW)))

        def split_factors(eng, n, b, in_turn=False):
            eng.wait_ge(fac_rounded[n], b + 1 + (n == 0))
            for i, (rows, cols) in enumerate(LO_PARTS):
                if i and in_turn:
                    eng.wait_ge(fac_ready[n], 3 * b + i)
                eng.tensor_tensor(fac[n][rows, cols], fac_raw[n][rows, cols], f(fac[n][rows, cols]),
                                  ALU.subtract).then_inc(fac_ready[n], 1)

        def split_x(eng, b, u):
            eng.wait_ge(x_rounded, b + 1)
            eng.tensor_tensor(x_lo[:, u, :], x_raw[:, u, :], f(x_hi[:, u, :]), ALU.subtract)\
                .then_inc(x_ready, 1)

        @block.vector
        def _(dve):
            def sum_w(n, j, done, done_n, raw, bank=ps_w, first=False):
                dve.wait_ge(done, done_n)
                if not first or j >= 2:
                    dve.wait_ge(w_ready, n - 1)
                dve.scalar_tensor_tensor(out=w_sum[:, j % 2, :], in0=bank[:, :], scalar=ALPHA, in1=raw[:, j, :],
                                         op0=ALU.mult, op1=ALU.add).then_inc(w_summed, 1)

            def lo_w(n, j, hi, lo):
                dve.wait_ge(w_rounded, n + 1)
                dve.tensor_tensor(lo[:, j, :], w_sum[:, j % 2, :], f(hi[:, j, :]), ALU.subtract)\
                    .then_inc(w_ready, 1)

            def lo_h(b, j):
                dve.wait_ge(h_rounded, NJ * b + j + 1)
                dve.scalar_tensor_tensor(out=h_lo[:, j, :], in0=ps_a[j % 2][:, :], scalar=0.0,
                                         in1=f(h_hi[:, j, :]), op0=ALU.max, op1=ALU.subtract)\
                    .then_inc(h_ready, 1)

            def lo_g(q, k):
                dve.wait_ge(g_rounded, FC * q + k + 1)
                dve.tensor_tensor(g_lo[:, k, :], g_full[:, k % 2, :], f(g_hi[:, k, :]), ALU.subtract)\
                    .then_inc(g_ready, 1)

            def sum_x1(b, u, p, first):
                dve.wait_ge(b_done, NJ * (b + 1))
                if not first:
                    dve.wait_ge(bias_added, 2 * p)
                dve.tensor_tensor(x1[:, :, u * T:(u + 1) * T], ps_b[:, :].rearrange("p (c t) -> p c t", c=DC),
                                  x_raw[:, u, :].rearrange("p (c t) -> p c t", c=DC), ALU.add)\
                    .then_inc(x1_summed, 1)

            def lo_x1(b, u):
                dve.wait_ge(x1_rounded, b + 1)
                t = slice(u * T, (u + 1) * T)
                dve.tensor_tensor(x1_lo[:, :, t], x1[:, :, t], f(x1_hi[:, :, t]), ALU.subtract)\
                    .then_inc(x1_ready, 1)

            def make_out(q):
                dve.wait_ge(bias_added, 2 * (q + 1))
                for c in range(DC):
                    dve.wait_ge(d_done, DC * FC * (q + 1) - DC + 1 + c)
                    dve.tensor_tensor(x1_bias[:, c, :], ps_d[c][:, :], x1_bias[:, c, :], ALU.add)\
                        .then_inc(out_made, 1)

            def step(p, block0=True, block1=True, first=False, last=False):
                for s in range(16):
                    u, j = s // 8, s % NJ
                    b = 2 * p + u
                    more = block0 and not (last and u == 1)
                    if block0 and s % 8 < NJ and not (first and s < NJ):
                        sum_w(8 * b + NJ + j, j, fold2_done, NJ * b + j + 1, wo_raw)
                    elif more and not (first and s < NJ):
                        sum_w(8 * b + 8 + j, j, fold1_done, NJ * (b + 1) + j + 1, wi_raw)
                    if block0 and s % 8 == 0:
                        lo_w(8 * b + NJ - 1, NJ - 1, w1_hi, w1_lo)
                    elif block0 and s % 8 <= NJ:
                        lo_w(8 * b + NJ + s % 8 - 1, s % 8 - 1, w2_hi, w2_lo)
                    elif more:
                        lo_w(8 * b + 8 + j - 1, j - 1, w1_hi, w1_lo)
                    if block1 and 1 <= s <= FC:
                        lo_g(p - 1, s - 1)
                    if block0 and s == 8:
                        sum_x1(b - 1, 0, p, first)
                    if block0 and s == 15:
                        sum_x1(b, 1, p, first)
                    if block0 and s % 8 < NJ:
                        lo_h(b, j)
                    if first and s < NJ:
                        if s == 0:
                            dve.wait_ge(in_wo, 16)
                        sum_w(8 * b + NJ + j, j, fold2_done, NJ * b + j + 1, wo_raw)
                    if block0 and s == 8:
                        lo_x1(b - 1, 0)
                    if block0 and s == 15:
                        lo_x1(b, 1)
                if block1:
                    make_out(p - 1)

            dve.memset(zero[:, :], 0.0).then_inc(zeroed, 1)
            dve.wait_ge(fac_rounded[0], 1)
            for rows, cols in (*LO_PARTS[:2], (LO_PARTS[2][0], slice(D, FIRST))):
                dve.tensor_tensor(fac[0][rows, cols], fac_raw[0][rows, cols], f(fac[0][rows, cols]),
                                  ALU.subtract).then_inc(first_ready, 1)
            dve.wait_ge(fac_rounded[0], 2)
            rows, cols = LO_PARTS[2][0], slice(FIRST, FACW)
            dve.tensor_tensor(fac[0][rows, cols], fac_raw[0][rows, cols], f(fac[0][rows, cols]),
                              ALU.subtract).then_inc(fac_ready[0], 3)
            split_x(dve, 0, 0)
            for j in range(NJ):
                dve.wait_ge(in_wi[j], 16)
                sum_w(j, j, fold1_done, j + 1, wi_raw, ps_first[j], True)
                if j:
                    lo_w(j - 1, j - 1, w1_hi, w1_lo)
            step(0, block1=False, first=True)
            with dve.Fori(1, PAIRS - 1) as p:
                step(p)
            step(PAIRS - 1, last=True)
            step(PAIRS, block0=False)

        @block.gpsimd
        def _(pool):
            def lo_fc1(j):
                pool.wait_ge(fc1_rounded, j + 1)
                k = slice(j * FJ, (j + 1) * FJ)
                pool.tensor_tensor(fc1_lo[:, k, :], fc_raw[:, j * FJ * D:(j + 1) * FJ * D]
                                  .rearrange("p (k n) -> p k n", k=FJ), f(fc1_hi[:, k, :]), ALU.subtract)\
                    .then_inc(fc1_ready, 1)
                pool.wait_ge(fc1_ready, j + 1)

            def lo_fc2():
                pool.wait_ge(fc2_rounded, 2)
                raw = fc_raw[:, 0:FC * SHARED].rearrange("p (k n) -> p k n", k=FC)
                pool.tensor_tensor(fc2_lo[:, :, 0:SHARED], raw, f(fc2_hi[:, :, 0:SHARED]), ALU.subtract)\
                    .then_inc(fc2_ready, 1)
                pool.wait_ge(fc2_ready, 1)
                pool.tensor_tensor(fc2_lo[:, :, D:D + PART], raw[:, :, P:SHARED], f(fc2_hi[:, :, D:D + PART]),
                                  ALU.subtract).then_inc(fc2_ready, 1)
                pool.wait_ge(fc2_ready, 2)

            def split_expert(q):
                for v in range(2):
                    pool.wait_ge(expert_rounded, 2 * q + 1 + v)
                    hi, lo = (expert_cols(t, v) for t in (fc2_hi, fc2_lo))
                    raw = expert_raw[:, v, 0:FC * PART].rearrange("p (k n) -> p k n", k=FC)
                    pool.tensor_tensor(lo, raw, f(hi), ALU.subtract).then_inc(expert_ready, 1)
                    pool.wait_ge(expert_ready, 2 * q + 1 + v)

            def step(p, block0=True, block1=True, last=False):
                for u in range(2):
                    b = 2 * p + u
                    more = block0 and not (last and u == 1)
                    if more:
                        split_factors(pool, 0, b + 1, True)
                        pool.wait_ge(fac_ready[0], 3 * (b + 2))
                        split_x(pool, b + 1, 1 - u)
                        pool.wait_ge(x_ready, b + 2)
                    if block1 and u == 0:
                        split_expert(p - 1)
                    if more:
                        split_factors(pool, 1, b + 1, True)
                        pool.wait_ge(fac_ready[1], 3 * (b + 2))
                    if not block1 and u == 0:
                        for j in range(NJ):
                            lo_fc1(j)
                    if not block1 and u == 1:
                        lo_fc2()

            split_factors(pool, 1, 0, True)
            pool.wait_ge(fac_ready[1], 3)
            step(0, block1=False)
            with pool.Fori(1, PAIRS - 1) as p:
                step(p)
            step(PAIRS - 1, last=True)
            step(PAIRS, block0=False)


def kernel(**inputs):
    import numpy as np
    import concourse.bacc as bacc
    from concourse.bass_utils import run_bass_kernel_spmd

    def get(name):
        return np.asarray(inputs[name])

    x = get("x").reshape(B, T, DC, P).transpose(0, 3, 2, 1).reshape(B, P, DC * T)
    wi = get("L0_cond_wi").reshape(NJ, FJ * P, DC, P).transpose(3, 0, 2, 1).reshape(P, NJ, DC * FJ * P)
    wo = get("L0_cond_wo").reshape(D, NJ, FJ, P).transpose(3, 1, 2, 0).reshape(P, NJ, FJ * D)
    fc1 = get("L1_cond_fc1_w").reshape(FC, P, DC, P).transpose(3, 0, 2, 1).reshape(P, FC * D)
    fc2 = get("L1_cond_fc2_w").reshape(SHARED, FC, P).transpose(2, 1, 0).reshape(P, FC * SHARED)
    common = np.stack([
        np.concatenate([get("L0_cond_common_wi_a"), get("L0_cond_common_wi_b").T], axis=1),
        np.concatenate([get("L0_cond_common_wo_b").T, get("L0_cond_common_wo_a")], axis=1)])
    expert = np.stack([
        np.concatenate([get("L0_cond_experts_wi_a"), get("L0_cond_experts_wi_b").transpose(0, 2, 1)], axis=2),
        np.concatenate([get("L0_cond_experts_wo_b").transpose(0, 2, 1), get("L0_cond_experts_wo_a")], axis=2)],
        axis=1)
    factors = np.concatenate([np.broadcast_to(common, expert.shape), expert], axis=2)
    ew = get("L1_cond_experts_w")
    n_experts = ew.shape[0]
    ew = ew.reshape(n_experts, PART, FC, P).transpose(0, 3, 2, 1).reshape(n_experts, P, FC * PART)
    b2 = get("L1_cond_fc2_b")
    bias = np.concatenate([np.broadcast_to(b2[P:], (n_experts, SHARED - P)), get("L1_cond_experts_b")], axis=1)
    ew = np.concatenate([ew, bias[:, :, None]], axis=2)

    arrays = {
        "x": x, "experts_in": ew, "factors": factors, "wi": wi, "wo": wo,
        "fc1": fc1, "fc2": fc2, "bias1": get("L1_cond_fc1_b").reshape(FC, P).T, "bias2": b2[:P].reshape(P, 1),
        "idx": np.concatenate([get("itok_B_0_7"), get("itok_B_0_15")]).reshape(1, 2 * B),
    }
    nc = bacc.Bacc("TRN2", target_bir_lowering=False, num_devices=1)
    feeds, args = {}, []
    for name, a in arrays.items():
        a = np.ascontiguousarray(a)
        feeds[f"{name}_dram"] = a
        args.append(nc.dram_tensor(f"{name}_dram", a.shape, mybir.dt.from_np(a.dtype), kind="ExternalInput").ap())
    args.append(nc.dram_tensor("out_dram", (PAIRS, P, DC * T2), mybir.dt.float32, kind="ExternalOutput").ap())
    program(nc, *args)
    r = run_bass_kernel_spmd(nc, [feeds], core_ids=[0])
    got = np.asarray(r.results[0]["out_dram"]).reshape(PAIRS, P, DC, 2, T)
    return got.transpose(0, 3, 4, 2, 1).reshape(B, T, D)
```

```python
from contextlib import ExitStack

import concourse.bass as bass
from concourse import mybir

P = 128
B, T, D = 8, 256, 256
F = 1024
RANK = 32
PART = 64
SHARED = D - PART
ALPHA = 2.0
DC = D // P
FC = F // P
NJ = 4
FJ = FC // NJ
PAIRS = B // 2
T2 = 2 * T
FACW = F + D
F2W = D + P
GROUPS = P // RANK
WARM_UP = 31
FIRST = D + FJ * P


def program(nc, x, experts_in, factors, wi, wo, fc1, fc2, bias1, bias2, idx, out):
    f32, f32r, i32 = mybir.dt.float32, mybir.dt.float32r, mybir.dt.int32
    ALU = mybir.AluOpType
    ACT = mybir.ActivationFunctionType

    with ExitStack() as ctx:
        def sb(name, shape, dt=f32):
            return ctx.enter_context(nc.sbuf_tensor(name, shape, dt))

        def pb(name):
            return ctx.enter_context(nc.psum_tensor(name, [P, 512], f32))

        def sem(name):
            return ctx.enter_context(nc.semaphore(name))

        def f(ap):
            return ap.bitcast(f32)

        idx_sb = sb("idx_sb", [1, 2 * B], i32)
        x_raw = sb("x_raw", [P, 2, DC * T])
        fac_raw = [sb(f"fac{n}_raw", [P, FACW]) for n in (1, 2)]
        wi_raw = sb("wi_raw", [P, NJ, DC * FJ * P])
        wo_raw = sb("wo_raw", [P, NJ, FJ * D])
        fc_raw = sb("fc_raw", [P, FC * D])
        expert_raw = sb("expert_raw", [P, 2, FC * PART + 1])
        bias1_sb = sb("bias1_sb", [P, FC])
        bias2_sb = sb("bias2_sb", [P, 1])
        x_hi, x_lo = (sb(f"x_{s}", [P, 2, DC * T], f32r) for s in ("hi", "lo"))
        fac = [sb(f"fac{n}", [P, FACW], f32r) for n in (1, 2)]
        w1_hi, w1_lo = (sb(f"w1_{s}", [P, NJ, DC * FJ * P], f32r) for s in ("hi", "lo"))
        w2_hi, w2_lo = (sb(f"w2_{s}", [P, NJ, FJ * D], f32r) for s in ("hi", "lo"))
        h_hi, h_lo = (sb(f"h_{s}", [P, NJ, FJ * T], f32r) for s in ("hi", "lo"))
        fc1_hi, fc1_lo = (sb(f"fc1_{s}", [P, FC, D], f32r) for s in ("hi", "lo"))
        fc2_hi, fc2_lo = (sb(f"fc2_{s}", [P, FC, F2W], f32r) for s in ("hi", "lo"))
        x1_hi, x1_lo = (sb(f"x1_{s}", [P, DC, T2], f32r) for s in ("hi", "lo"))
        g_hi, g_lo = (sb(f"g_{s}", [P, FC, T2], f32r) for s in ("hi", "lo"))
        zero = sb("zero", [P, 512], mybir.dt.bfloat16)
        scratch = sb("scratch", [P, 1])
        w_sum = sb("w_sum", [P, 2, 512])
        g_full = sb("g_full", [P, 2, T2])
        x1 = sb("x1", [P, DC, T2])
        x1_bias = sb("x1_bias", [P, DC, T2])

        ps_w = pb("ps_w")
        ps_a = [pb("ps_a0"), pb("ps_a1")]
        ps_b = pb("ps_b")
        ps_c = [pb("ps_c0"), pb("ps_c1")]
        ps_d = [pb("ps_d0"), pb("ps_d1")]
        ps_first = [ps_w, ps_c[0], ps_c[1], ps_d[1]]

        in_idx = sem("in_idx")
        zeroed = sem("zeroed")
        in_x = [sem("in_x0"), sem("in_x1")]
        in_fac = [sem("in_fac1"), sem("in_fac2")]
        in_wi = [sem(f"in_wi{j}") for j in range(NJ)]
        in_wo = sem("in_wo")
        in_fc1 = sem("in_fc1")
        in_fc2 = sem("in_fc2")
        in_expert = sem("in_expert")
        in_bias = sem("in_bias")
        out_stored = sem("out_stored")
        fold1_done = sem("fold1_done")
        fold2_done = sem("fold2_done")
        a_done = sem("a_done")
        b_done = sem("b_done")
        c_done = sem("c_done")
        d_done = sem("d_done")
        fac_rounded = [sem("fac1_rounded"), sem("fac2_rounded")]
        first_ready = sem("first_ready")
        fac_ready = [sem("fac1_ready"), sem("fac2_ready")]
        x_rounded, x_ready = sem("x_rounded"), sem("x_ready")
        w_summed, w_rounded, w_ready = sem("w_summed"), sem("w_rounded"), sem("w_ready")
        h_rounded, h_ready = sem("h_rounded"), sem("h_ready")
        x1_summed, x1_rounded, x1_ready = sem("x1_summed"), sem("x1_rounded"), sem("x1_ready")
        g_made, g_rounded, g_ready = sem("g_made"), sem("g_rounded"), sem("g_ready")
        fc1_rounded, fc1_ready = sem("fc1_rounded"), sem("fc1_ready")
        fc2_rounded, fc2_ready = sem("fc2_rounded"), sem("fc2_ready")
        expert_rounded, expert_ready = sem("expert_rounded"), sem("expert_ready")
        bias_added = sem("bias_added")
        out_made = sem("out_made")

        def expert_cols(t, v):
            return t[:, :, (1 + v) * P + PART:(2 + v) * P]

        block = ctx.enter_context(nc.Block())

        @block.sync
        def _(sp):
            def load_factors(n, row, first=False):
                skip = 0 if first else RANK // 2
                for g in range(GROUPS):
                    sp.dma_start(fac_raw[n][g * RANK + skip:(g + 1) * RANK, :],
                                 factors[bass.ds(row, 1), n, skip:RANK, :].rearrange("a r n -> (a r) n"))\
                        .then_inc(in_fac[n], 16)

            def load_x(b, u):
                sp.dma_start(x_raw[:, u, :], x[bass.ds(b, 1), :, :].rearrange("a p n -> (a p) n"))\
                    .then_inc(in_x[u], 16)

            def load_expert(p, u, row):
                sp.dma_start(expert_raw[:, u, :],
                             experts_in[bass.ds(row, 1), :, :].rearrange("a p n -> (a p) n"))\
                    .then_inc(in_expert, 16)

            def row0(b):
                return sp.value_load(idx_sb[0:1, bass.ds(b, 1)], min_val=0, max_val=factors.shape[0] - 1)

            def row1(b):
                return sp.value_load(idx_sb[0:1, bass.ds(b + B, 1)], min_val=0, max_val=experts_in.shape[0] - 1)

            def store(q):
                for c in range(DC):
                    sp.wait_ge(out_made, DC * q + c + 1)
                    sp.dma_start(out[bass.ds(q, 1), :, c * T2:(c + 1) * T2].rearrange("a p n -> (a p) n"),
                                 x1_bias[:, c, :]).then_inc(out_stored, 16)

            def step(p, block1=True, last=False):
                for u in range(2):
                    b = 2 * p + u
                    if not last:
                        row = row0(b + 2)
                        sp.wait_ge(fac_ready[0], 3 * (b + 2))
                        load_factors(0, row)
                    if u == 0 and block1:
                        rows = [row1(2 * p + v) for v in range(2)]
                        sp.wait_ge(expert_ready, 2 * p)
                        sp.wait_ge(bias_added, 2 * p)
                        for v in range(2):
                            load_expert(p, v, rows[v])
                    if not last:
                        sp.wait_ge(fac_ready[1], 3 * (b + 2))
                        load_factors(1, row)
                        sp.wait_ge(x1_summed, b + 1)
                        load_x(b + 2, u)
                    if u == 0 and not block1:
                        sp.wait_ge(fc1_ready, NJ)
                        sp.dma_start(fc_raw[:, 0:FC * SHARED], fc2).then_inc(in_fc2, 16)
                if block1:
                    store(p - 1)

            sp.dma_start(idx_sb[:, :], idx).then_inc(in_idx, 16)
            sp.wait_ge(in_idx, 16)
            row = row0(0)
            load_factors(0, row, first=True)
            load_factors(1, row, first=True)
            sp.dma_start(wo_raw[:, :, :], wo).then_inc(in_wo, 16)
            row = row0(1)
            sp.wait_ge(fac_ready[0], 3)
            load_factors(0, row)
            load_x(1, 1)
            sp.wait_ge(fac_ready[1], 3)
            load_factors(1, row)
            sp.dma_start(fc_raw[:, :], fc1).then_inc(in_fc1, 16)
            sp.dma_start(bias1_sb[:, :], bias1).then_inc(in_bias, 16)
            sp.dma_start(bias2_sb[:, :], bias2).then_inc(in_bias, 16)
            for u in range(2):
                load_expert(0, u, row1(u))
            step(0, block1=False)
            with sp.Fori(1, PAIRS - 1) as p:
                step(p)
            step(PAIRS - 1, last=True)
            store(PAIRS - 1)
            sp.wait_ge(out_stored, 32 * (PAIRS + 1))

        @block.tensor
        def _(pe):
            def products(acc, w, v, start, stop):
                pe.matmul(acc, w[0], v[0], start=start, stop=False, skip_group_check=True)
                pe.matmul(acc, w[0], v[1], start=False, stop=False, skip_group_check=True)
                return pe.matmul(acc, w[1], v[0], start=False, stop=stop, skip_group_check=True)

            def fold1(b, j, bank=None):
                if bank is ps_first[0]:
                    pe.wait_ge(first_ready, 3)
                elif j == 0 or bank is ps_first[1]:
                    pe.wait_ge(fac_ready[0], 3 * (b + 1))
                if bank is None:
                    bank = ps_w
                    pe.wait_ge(w_summed, 8 * b + j)
                v = slice(D + j * FJ * P, D + (j + 1) * FJ * P)
                for c in range(DC):
                    mm = pe.matmul(bank[:, c * FJ * P:(c + 1) * FJ * P], fac[0][:, c * P:(c + 1) * P],
                                   fac[0][:, v], start=True, stop=True)
                mm.then_inc(fold1_done, 1)

            def fold2(b, j):
                if j == 0:
                    pe.wait_ge(fac_ready[1], 3 * (b + 1))
                pe.wait_ge(w_summed, 8 * b + NJ + j)
                for i in range(FJ):
                    k = j * FJ + i
                    mm = pe.matmul(ps_w[:, i * D:(i + 1) * D], fac[1][:, D + k * P:D + (k + 1) * P],
                                   fac[1][:, 0:D], start=True, stop=True)
                mm.then_inc(fold2_done, 1)

            def unit_a(b, u, j):
                if j == 0:
                    pe.wait_ge(x_ready, b + 1)
                pe.wait_ge(w_ready, 8 * b + j + 1)
                if j >= 2:
                    pe.wait_ge(h_ready, NJ * b + j - 1)
                for i in range(FJ):
                    for c in range(DC):
                        w = slice((c * FJ + i) * P, (c * FJ + i + 1) * P)
                        v = slice(c * T, (c + 1) * T)
                        mm = products(ps_a[j % 2][:, i * T:(i + 1) * T], (w1_hi[:, j, w], w1_lo[:, j, w]),
                                      (x_hi[:, u, v], x_lo[:, u, v]), c == 0, c == DC - 1)
                mm.then_inc(a_done, 1)

            def unit_b(b, j, first):
                if j == 0 and not first:
                    pe.wait_ge(x1_summed, b)
                pe.wait_ge(w_ready, 8 * b + NJ + j + 1)
                pe.wait_ge(h_ready, NJ * b + j + 1)
                for i in range(FJ):
                    for c in range(DC):
                        w = slice(i * D + c * P, i * D + (c + 1) * P)
                        v = slice(i * T, (i + 1) * T)
                        mm = products(ps_b[:, c * T:(c + 1) * T], (w2_hi[:, j, w], w2_lo[:, j, w]),
                                      (h_hi[:, j, v], h_lo[:, j, v]), j == i == c == 0,
                                      j == NJ - 1 and i == FJ - 1)
                mm.then_inc(b_done, 1)

            def unit_c(q, k):
                if k == 0:
                    pe.wait_ge(x1_ready, 2 * q + 2)
                    pe.wait_ge(fc1_ready, NJ)
                if k >= 2:
                    pe.wait_ge(g_made, FC * q + k - 1)
                for c in range(DC):
                    w = slice(c * P, (c + 1) * P)
                    mm = products(ps_c[k % 2][:, :], (fc1_hi[:, k, w], fc1_lo[:, k, w]),
                                  (x1_hi[:, c, :], x1_lo[:, c, :]), c == 0, c == DC - 1)
                mm.then_inc(c_done, 1)

            def unit_d(q, k):
                if k == 0:
                    pe.wait_ge(expert_ready, 2 * q + 2)
                    pe.wait_ge(fc2_ready, 2)
                pe.wait_ge(g_ready, FC * q + k + 1)
                mm = products(ps_d[0][:, :], (fc2_hi[:, k, 0:P], fc2_lo[:, k, 0:P]),
                              (g_hi[:, k, :], g_lo[:, k, :]), k == 0, k == FC - 1)
                mm.then_inc(d_done, 1)
                for v in range(2):
                    w = slice((1 + v) * P, (2 + v) * P)
                    t = slice(v * T, (v + 1) * T)
                    mm = products(ps_d[1][:, t], (fc2_hi[:, k, w], fc2_lo[:, k, w]),
                                  (g_hi[:, k, t], g_lo[:, k, t]), k == v == 0, k == FC - 1)
                mm.then_inc(d_done, 1)

            def step(p, block0=True, block1=True, first=False, last=False):
                for s in range(16):
                    u, j = s // 8, s % NJ
                    b = 2 * p + u
                    if first and s < NJ:
                        unit_a(b, u, j)
                        if s:
                            fold2(b, j - 1)
                    elif block0 and s % 8 < NJ:
                        fold2(b, j)
                        unit_a(b, u, j)
                    elif block0:
                        if first and s == NJ:
                            fold2(b, NJ - 1)
                        if not (last and u == 1):
                            fold1(b + 1, j)
                        unit_b(b, j, first and u == 0)
                    if block1 and s < FC:
                        unit_c(p - 1, s)
                    elif block1 and last and s == 14:
                        continue
                    elif block1:
                        if last and s == 15:
                            unit_d(p - 1, 6)
                        unit_d(p - 1, s - FC)

            pe.wait_ge(zeroed, 1)
            for _ in range(WARM_UP):
                pe.matmul(ps_a[1][:, :], zero[:, 0:P], zero[:, :], start=True, stop=True)
            for j in range(NJ):
                fold1(0, j, ps_first[j])
            step(0, block1=False, first=True)
            with pe.Fori(1, PAIRS - 1) as p:
                step(p)
            step(PAIRS - 1, last=True)
            step(PAIRS, block0=False)

        @block.scalar
        def _(act):
            def round_factors(n, b, first=False, cols=slice(0, FACW)):
                act.wait_ge(in_fac[n], 16 * GROUPS * (b + 1))
                if not first:
                    act.wait_ge(fold1_done if n == 0 else fold2_done, NJ * b)
                act.activation(fac[n][:, cols], fac_raw[n][:, cols], ACT.Copy).then_inc(fac_rounded[n], 1)

            def round_x(b, u, p, first=False):
                act.wait_ge(in_x[u], 16 * (p + 1))
                if not first:
                    act.wait_ge(a_done, NJ * (b - 1))
                act.activation(x_hi[:, u, :], x_raw[:, u, :], ACT.Copy).then_inc(x_rounded, 1)

            def round_w(n, j, dst):
                act.wait_ge(w_summed, n + 1)
                act.activation(dst[:, j, :], w_sum[:, j % 2, :], ACT.Copy).then_inc(w_rounded, 1)

            def relu(b, j):
                act.wait_ge(a_done, NJ * b + j + 1)
                act.activation(h_hi[:, j, :], ps_a[j % 2][:, :], ACT.Relu).then_inc(h_rounded, 1)

            def gelu(q, k):
                act.wait_ge(c_done, FC * q + k + 1)
                if k >= 2:
                    act.wait_ge(g_ready, FC * q + k - 1)
                act.activation(g_full[:, k % 2, :], ps_c[k % 2][:, :], ACT.Gelu, bias=bias1_sb[:, k:k + 1])\
                    .then_inc(g_made, 1)
                act.wait_ge(g_made, FC * q + k + 1)
                act.activation(g_hi[:, k, :], g_full[:, k % 2, :], ACT.Copy).then_inc(g_rounded, 1)

            def round_expert(q):
                act.wait_ge(in_expert, 32 * (q + 1))
                for v in range(2):
                    raw = expert_raw[:, v, 0:FC * PART].rearrange("p (k n) -> p k n", k=FC)
                    act.activation(expert_cols(fc2_hi, v), raw, ACT.Copy).then_inc(expert_rounded, 1)

            def add_bias(q):
                act.wait_ge(x1_summed, 2 * q + 2)
                act.wait_ge(out_stored, 32 * (q + 1))
                act.activation(x1_bias[:, 0, :], x1[:, 0, :], ACT.Identity, bias=bias2_sb[:, 0:1])\
                    .then_inc(bias_added, 1)
                for v in range(2):
                    t = slice(v * T, (v + 1) * T)
                    op = act.activation(x1_bias[:, 1, t], x1[:, 1, t], ACT.Identity,
                                        bias=expert_raw[:, v, FC * PART:FC * PART + 1])
                op.then_inc(bias_added, 1)

            def round_x1(b, u, p, first):
                act.wait_ge(x1_summed, b + 1)
                if not first:
                    act.wait_ge(c_done, FC * p)
                t = slice(u * T, (u + 1) * T)
                act.activation(x1_hi[:, :, t], x1[:, :, t], ACT.Copy).then_inc(x1_rounded, 1)

            def round_fc1(j):
                act.wait_ge(in_fc1, 16)
                k = slice(j * FJ, (j + 1) * FJ)
                act.activation(fc1_hi[:, k, :], fc_raw[:, j * FJ * D:(j + 1) * FJ * D]
                               .rearrange("p (k n) -> p k n", k=FJ), ACT.Copy).then_inc(fc1_rounded, 1)

            def round_fc2(part):
                act.wait_ge(in_fc2, 16)
                raw = fc_raw[:, 0:FC * SHARED].rearrange("p (k n) -> p k n", k=FC)
                if part < 2:
                    k = slice(part * FC // 2, (part + 1) * FC // 2)
                    act.activation(fc2_hi[:, k, 0:SHARED], raw[:, k, :], ACT.Copy).then_inc(fc2_rounded, 1)
                else:
                    act.activation(fc2_hi[:, :, D:D + PART], raw[:, :, P:SHARED], ACT.Copy)\
                        .then_inc(fc2_rounded, 1)

            def step(p, block0=True, block1=True, first=False, last=False):
                for s in range(16):
                    u, j = s // 8, s % NJ
                    b = 2 * p + u
                    more = block0 and not (last and u == 1)
                    if block1 and 1 <= s <= FC:
                        gelu(p - 1, s - 1)
                    if first and s == 8:
                        round_factors(0, b + 1)
                    if block0 and block1 and s == 2:
                        round_expert(p - 1)
                    if block0 and block1 and s == 5:
                        add_bias(p - 1)
                    if first and s <= NJ:
                        if s < NJ:
                            relu(b, j)
                        if s:
                            round_w(8 * b + NJ + s - 1, s - 1, w2_hi)
                    elif block0 and s % 8 < NJ:
                        relu(b, j)
                        round_w(8 * b + NJ + j, j, w2_hi)
                    if more and s % 8 >= NJ:
                        round_w(8 * b + 8 + j, j, w1_hi)
                    if block0 and s == 8:
                        round_x1(b - 1, 0, p, first)
                    if block0 and s == 15:
                        round_x1(b, 1, p, first)
                    if more and s % 8 == 0 and not (first and s == 8):
                        round_factors(0, b + 1)
                    if more and s % 8 == 2:
                        round_x(b + 1, 1 - u, p + u, first and u == 0)
                    if more and s % 8 == 4:
                        round_factors(1, b + 1)
                    if first and 4 <= s < 8:
                        round_fc1(j)
                    if first and s >= 13:
                        round_fc2(s - 13)

            act.nop().then_inc(out_stored, 32)
            act.dma_start(x_raw[:, 0, :], x[0, :, :]).then_inc(in_x[0], 16)
            for j in range(NJ):
                act.dma_start(wi_raw[:, j, :], wi[:, j, :]).then_inc(in_wi[j], 16)
            act.wait_ge(zeroed, 1)
            act.activation(scratch[:, :], zero[:, 0:1], ACT.Gelu)
            round_factors(0, 0, True, slice(0, FIRST))
            round_factors(0, 0, True, slice(FIRST, FACW))
            round_x(0, 0, 0, True)
            round_w(0, 0, w1_hi)
            round_w(1, 1, w1_hi)
            round_factors(1, 0, True)
            round_w(2, 2, w1_hi)
            round_w(3, 3, w1_hi)
            step(0, block1=False, first=True)
            act.wait_ge(in_bias, 32)
            with act.Fori(1, PAIRS - 1) as p:
                step(p)
            step(PAIRS - 1, last=True)
            step(PAIRS, block0=False)

        LO_PARTS = ((slice(RANK, 2 * RANK), slice(0, D)), (slice(3 * RANK, P), slice(0, D)),
                    (slice(2 * RANK, P), slice(D, FACW)))

        def split_factors(eng, n, b, in_turn=False):
            eng.wait_ge(fac_rounded[n], b + 1 + (n == 0))
            for i, (rows, cols) in enumerate(LO_PARTS):
                if i and in_turn:
                    eng.wait_ge(fac_ready[n], 3 * b + i)
                eng.tensor_tensor(fac[n][rows, cols], fac_raw[n][rows, cols], f(fac[n][rows, cols]),
                                  ALU.subtract).then_inc(fac_ready[n], 1)

        def split_x(eng, b, u):
            eng.wait_ge(x_rounded, b + 1)
            eng.tensor_tensor(x_lo[:, u, :], x_raw[:, u, :], f(x_hi[:, u, :]), ALU.subtract)\
                .then_inc(x_ready, 1)

        @block.vector
        def _(dve):
            def sum_w(n, j, done, done_n, raw, bank=ps_w, first=False):
                dve.wait_ge(done, done_n)
                if not first or j >= 2:
                    dve.wait_ge(w_ready, n - 1)
                dve.scalar_tensor_tensor(out=w_sum[:, j % 2, :], in0=bank[:, :], scalar=ALPHA, in1=raw[:, j, :],
                                         op0=ALU.mult, op1=ALU.add).then_inc(w_summed, 1)

            def lo_w(n, j, hi, lo):
                dve.wait_ge(w_rounded, n + 1)
                dve.tensor_tensor(lo[:, j, :], w_sum[:, j % 2, :], f(hi[:, j, :]), ALU.subtract)\
                    .then_inc(w_ready, 1)

            def lo_h(b, j):
                dve.wait_ge(h_rounded, NJ * b + j + 1)
                dve.scalar_tensor_tensor(out=h_lo[:, j, :], in0=ps_a[j % 2][:, :], scalar=0.0,
                                         in1=f(h_hi[:, j, :]), op0=ALU.max, op1=ALU.subtract)\
                    .then_inc(h_ready, 1)

            def lo_g(q, k):
                dve.wait_ge(g_rounded, FC * q + k + 1)
                dve.tensor_tensor(g_lo[:, k, :], g_full[:, k % 2, :], f(g_hi[:, k, :]), ALU.subtract)\
                    .then_inc(g_ready, 1)

            def sum_x1(b, u, p, first):
                dve.wait_ge(b_done, NJ * (b + 1))
                if not first:
                    dve.wait_ge(bias_added, 2 * p)
                dve.tensor_tensor(x1[:, :, u * T:(u + 1) * T], ps_b[:, :].rearrange("p (c t) -> p c t", c=DC),
                                  x_raw[:, u, :].rearrange("p (c t) -> p c t", c=DC), ALU.add)\
                    .then_inc(x1_summed, 1)

            def lo_x1(n, u):
                dve.wait_ge(x1_rounded, n)
                t = slice(u * T, (u + 1) * T)
                dve.tensor_tensor(x1_lo[:, :, t], x1[:, :, t], f(x1_hi[:, :, t]), ALU.subtract)\
                    .then_inc(x1_ready, 1)

            def make_out(q):
                dve.wait_ge(bias_added, 2 * (q + 1))
                for c in range(DC):
                    dve.wait_ge(d_done, DC * FC * (q + 1) - DC + 1 + c)
                    dve.tensor_tensor(x1_bias[:, c, :], ps_d[c][:, :], x1_bias[:, c, :], ALU.add)\
                        .then_inc(out_made, 1)

            def lo_fc1(j):
                dve.wait_ge(fc1_rounded, j + 1)
                k = slice(j * FJ, (j + 1) * FJ)
                dve.tensor_tensor(fc1_lo[:, k, :], fc_raw[:, j * FJ * D:(j + 1) * FJ * D]
                                  .rearrange("p (k n) -> p k n", k=FJ), f(fc1_hi[:, k, :]), ALU.subtract)\
                    .then_inc(fc1_ready, 1)

            def round_expert(q):
                dve.wait_ge(in_expert, 32 * (q + 1))
                dve.wait_ge(c_done, FC * q + 1)
                for v in range(2):
                    raw = expert_raw[:, v, 0:FC * PART].rearrange("p (k n) -> p k n", k=FC)
                    dve.tensor_copy(expert_cols(fc2_hi, v), raw).then_inc(expert_rounded, 1)

            def add_bias(q):
                dve.wait_ge(x1_summed, 2 * q + 2)
                dve.wait_ge(out_stored, 32 * (q + 1))
                dve.tensor_scalar(x1_bias[:, 0, :], x1[:, 0, :], bias2_sb[:, 0:1], None, ALU.add)\
                    .then_inc(bias_added, 1)
                for v in range(2):
                    t = slice(v * T, (v + 1) * T)
                    op = dve.tensor_scalar(x1_bias[:, 1, t], x1[:, 1, t],
                                           expert_raw[:, v, FC * PART:FC * PART + 1], None, ALU.add)
                op.then_inc(bias_added, 1)

            def step(p, block0=True, block1=True, first=False, last=False):
                for s in range(16):
                    u, j = s // 8, s % NJ
                    b = 2 * p + u
                    more = block0 and not (last and u == 1)
                    if not block0 and s == 1:
                        round_expert(p - 1)
                    if not block0 and s == 11:
                        add_bias(p - 1)
                    if first and 1 <= s <= NJ:
                        lo_h(b, s - 1)
                        if s == 1:
                            dve.wait_ge(in_wo, 16)
                        sum_w(8 * b + NJ + s - 1, s - 1, fold2_done, NJ * b + s, wo_raw)
                        if s == NJ:
                            lo_w(8 * b + NJ + NJ - 2, NJ - 2, w2_hi, w2_lo)
                    elif block0 and s % 8 < NJ and not (first and s == 0):
                        sum_w(8 * b + NJ + j, j, fold2_done, NJ * b + j + 1, wo_raw)
                    if more and s % 8 >= NJ:
                        sum_w(8 * b + 8 + j, j, fold1_done, NJ * (b + 1) + j + 1, wi_raw)
                    if block0 and 1 <= s % 8 <= NJ and not (first and s <= NJ):
                        lo_h(b, s % 8 - 1)
                    if block0 and s % 8 == 0:
                        lo_w(8 * b + NJ - 1, NJ - 1, w1_hi, w1_lo)
                    elif first and s <= NJ:
                        if 2 <= s < NJ:
                            lo_w(8 * b + NJ + s - 2, s - 2, w2_hi, w2_lo)
                        if s == NJ:
                            lo_w(8 * b + NJ + NJ - 1, NJ - 1, w2_hi, w2_lo)
                    elif block0 and s % 8 <= NJ:
                        lo_w(8 * b + NJ + s % 8 - 1, s % 8 - 1, w2_hi, w2_lo)
                    elif more:
                        lo_w(8 * b + 8 + j - 1, j - 1, w1_hi, w1_lo)
                    if first and s == 5:
                        lo_fc1(0)
                    if block1 and 1 <= s <= FC:
                        lo_g(p - 1, s - 1)
                    if block0 and s == 8:
                        sum_x1(b - 1, 0, p, first)
                    if block0 and s == 13:
                        lo_x1(b, 0)
                    if block0 and s == 15:
                        sum_x1(b, 1, p, first)
                        lo_x1(b + 1, 1)
                if block1:
                    make_out(p - 1)

            dve.memset(zero[:, :], 0.0).then_inc(zeroed, 1)
            dve.wait_ge(fac_rounded[0], 1)
            for rows, cols in (*LO_PARTS[:2], (LO_PARTS[2][0], slice(D, FIRST))):
                dve.tensor_tensor(fac[0][rows, cols], fac_raw[0][rows, cols], f(fac[0][rows, cols]),
                                  ALU.subtract).then_inc(first_ready, 1)
            dve.wait_ge(fac_rounded[0], 2)
            rows, cols = LO_PARTS[2][0], slice(FIRST, FACW)
            dve.tensor_tensor(fac[0][rows, cols], fac_raw[0][rows, cols], f(fac[0][rows, cols]),
                              ALU.subtract).then_inc(fac_ready[0], 3)
            for j in range(NJ):
                dve.wait_ge(in_wi[j], 16)
                sum_w(j, j, fold1_done, j + 1, wi_raw, ps_first[j], True)
                if j:
                    lo_w(j - 1, j - 1, w1_hi, w1_lo)
            dve.wait_ge(fac_rounded[1], 1)
            for rows, cols in LO_PARTS[:2]:
                dve.tensor_tensor(fac[1][rows, cols], fac_raw[1][rows, cols], f(fac[1][rows, cols]),
                                  ALU.subtract).then_inc(fac_ready[1], 1)
            step(0, block1=False, first=True)
            with dve.Fori(1, PAIRS - 1) as p:
                step(p)
            step(PAIRS - 1, last=True)
            step(PAIRS, block0=False)

        @block.gpsimd
        def _(pool):
            def lo_fc1(j):
                pool.wait_ge(fc1_rounded, j + 1)
                k = slice(j * FJ, (j + 1) * FJ)
                pool.tensor_tensor(fc1_lo[:, k, :], fc_raw[:, j * FJ * D:(j + 1) * FJ * D]
                                  .rearrange("p (k n) -> p k n", k=FJ), f(fc1_hi[:, k, :]), ALU.subtract)\
                    .then_inc(fc1_ready, 1)
                pool.wait_ge(fc1_ready, j + 1)

            def lo_fc2():
                pool.wait_ge(fc2_rounded, 3)
                raw = fc_raw[:, 0:FC * SHARED].rearrange("p (k n) -> p k n", k=FC)
                pool.tensor_tensor(fc2_lo[:, :, 0:SHARED], raw, f(fc2_hi[:, :, 0:SHARED]), ALU.subtract)\
                    .then_inc(fc2_ready, 1)
                pool.wait_ge(fc2_ready, 1)
                pool.tensor_tensor(fc2_lo[:, :, D:D + PART], raw[:, :, P:SHARED], f(fc2_hi[:, :, D:D + PART]),
                                  ALU.subtract).then_inc(fc2_ready, 1)
                pool.wait_ge(fc2_ready, 2)

            def split_expert(q):
                for v in range(2):
                    pool.wait_ge(expert_rounded, 2 * q + 1 + v)
                    hi, lo = (expert_cols(t, v) for t in (fc2_hi, fc2_lo))
                    raw = expert_raw[:, v, 0:FC * PART].rearrange("p (k n) -> p k n", k=FC)
                    pool.tensor_tensor(lo, raw, f(hi), ALU.subtract).then_inc(expert_ready, 1)
                    pool.wait_ge(expert_ready, 2 * q + 1 + v)

            def step(p, block0=True, block1=True, last=False):
                for u in range(2):
                    b = 2 * p + u
                    more = block0 and not (last and u == 1)
                    if more:
                        split_factors(pool, 0, b + 1, True)
                        pool.wait_ge(fac_ready[0], 3 * (b + 2))
                        split_x(pool, b + 1, 1 - u)
                        pool.wait_ge(x_ready, b + 2)
                    if block1 and u == 0:
                        split_expert(p - 1)
                    if more:
                        split_factors(pool, 1, b + 1, True)
                        pool.wait_ge(fac_ready[1], 3 * (b + 2))
                    if not block1 and u == 0:
                        for j in range(1, NJ):
                            lo_fc1(j)
                    if not block1 and u == 1:
                        lo_fc2()

            split_x(pool, 0, 0)
            pool.wait_ge(x_ready, 1)
            pool.wait_ge(fac_rounded[1], 1)
            rows, cols = LO_PARTS[2]
            pool.tensor_tensor(fac[1][rows, cols], fac_raw[1][rows, cols], f(fac[1][rows, cols]),
                               ALU.subtract).then_inc(fac_ready[1], 1)
            pool.wait_ge(fac_ready[1], 3)
            step(0, block1=False)
            with pool.Fori(1, PAIRS - 1) as p:
                step(p)
            step(PAIRS - 1, last=True)
            step(PAIRS, block0=False)


def kernel(**inputs):
    import numpy as np
    import concourse.bacc as bacc
    from concourse.bass_utils import run_bass_kernel_spmd

    def get(name):
        return np.asarray(inputs[name])

    x = get("x").reshape(B, T, DC, P).transpose(0, 3, 2, 1).reshape(B, P, DC * T)
    wi = get("L0_cond_wi").reshape(NJ, FJ * P, DC, P).transpose(3, 0, 2, 1).reshape(P, NJ, DC * FJ * P)
    wo = get("L0_cond_wo").reshape(D, NJ, FJ, P).transpose(3, 1, 2, 0).reshape(P, NJ, FJ * D)
    fc1 = get("L1_cond_fc1_w").reshape(FC, P, DC, P).transpose(3, 0, 2, 1).reshape(P, FC * D)
    fc2 = get("L1_cond_fc2_w").reshape(SHARED, FC, P).transpose(2, 1, 0).reshape(P, FC * SHARED)
    common = np.stack([
        np.concatenate([get("L0_cond_common_wi_a"), get("L0_cond_common_wi_b").T], axis=1),
        np.concatenate([get("L0_cond_common_wo_b").T, get("L0_cond_common_wo_a")], axis=1)])
    expert = np.stack([
        np.concatenate([get("L0_cond_experts_wi_a"), get("L0_cond_experts_wi_b").transpose(0, 2, 1)], axis=2),
        np.concatenate([get("L0_cond_experts_wo_b").transpose(0, 2, 1), get("L0_cond_experts_wo_a")], axis=2)],
        axis=1)
    factors = np.concatenate([np.broadcast_to(common, expert.shape), expert], axis=2)
    ew = get("L1_cond_experts_w")
    n_experts = ew.shape[0]
    ew = ew.reshape(n_experts, PART, FC, P).transpose(0, 3, 2, 1).reshape(n_experts, P, FC * PART)
    b2 = get("L1_cond_fc2_b")
    bias = np.concatenate([np.broadcast_to(b2[P:], (n_experts, SHARED - P)), get("L1_cond_experts_b")], axis=1)
    ew = np.concatenate([ew, bias[:, :, None]], axis=2)

    arrays = {
        "x": x, "experts_in": ew, "factors": factors, "wi": wi, "wo": wo,
        "fc1": fc1, "fc2": fc2, "bias1": get("L1_cond_fc1_b").reshape(FC, P).T, "bias2": b2[:P].reshape(P, 1),
        "idx": np.concatenate([get("itok_B_0_7"), get("itok_B_0_15")]).reshape(1, 2 * B),
    }
    nc = bacc.Bacc("TRN2", target_bir_lowering=False, num_devices=1)
    feeds, args = {}, []
    for name, a in arrays.items():
        a = np.ascontiguousarray(a)
        feeds[f"{name}_dram"] = a
        args.append(nc.dram_tensor(f"{name}_dram", a.shape, mybir.dt.from_np(a.dtype), kind="ExternalInput").ap())
    args.append(nc.dram_tensor("out_dram", (PAIRS, P, DC * T2), mybir.dt.float32, kind="ExternalOutput").ap())
    program(nc, *args)
    r = run_bass_kernel_spmd(nc, [feeds], core_ids=[0])
    got = np.asarray(r.results[0]["out_dram"]).reshape(PAIRS, P, DC, 2, T)
    return got.transpose(0, 3, 4, 2, 1).reshape(B, T, D)
```
